# Optimizing a Trainium2 kernel written in Bass

```python
import numpy as np
import jax
import jax.numpy as jnp

def _softmax(x, axis=-1):
    return jax.nn.softmax(x, axis=axis)

def _gelu(x):
    return jax.nn.gelu(x, approximate=True)

def _silu(x):
    return jax.nn.silu(x)

def _sigmoid(x):
    return jax.nn.sigmoid(x)

def _layernorm(x, axis=-1, eps=1e-05):
    m = jnp.mean(x, axis=axis, keepdims=True)
    v = jnp.var(x, axis=axis, keepdims=True)
    return (x - m) / jnp.sqrt(v + eps)

def _scatter_add(tgt, idx, src, axis=0):
    return tgt.at[idx].add(src)

def _segment_sum(src, seg, n):
    return jax.ops.segment_sum(src, seg, n)
kernel_name = 'mk_adj_resnorm_d4_adj_r2_29c656'

def setup_inputs(seed: int=0):
    np.random.seed(seed)
    _w = jnp.asarray

    def _rec_inputs():
        import jax
        import jax.numpy as jnp
        _gk = jax.random.key(seed)
        x = -0.0002928 + 1 * jax.random.normal(jax.random.fold_in(_gk, 1), (16, 512, 128), jnp.float32)
        _w = (1.0 + jnp.arange(512, dtype=jnp.float32)) ** (-0.5)
        _w = _w / _w.mean()
        _pij = jnp.clip(0.0078125 * _w[:, None] * _w[None, :], 0.0, 1.0)
        _a = jax.random.uniform(jax.random.fold_in(_gk, 2), (512, 512)) < _pij
        _a = jnp.logical_or(_a, jnp.swapaxes(_a, -1, -2))
        _a = jnp.logical_or(_a, jnp.eye(512, dtype=bool))
        _af = _a.astype(jnp.float32)
        _af = _af * jax.random.uniform(jax.random.fold_in(_gk, 3), (512, 512), jnp.float32, 0.05, 1)
        adj = _af
        return (x, adj)
    x, adj = _rec_inputs()

    def _L0_gnn_setup():
        import jax, jax.numpy as jnp
        import numpy as np
        B, N, D = (32, 512, 128)
        TIME_STEP = 5
        key = jax.random.key(seed)
        ks = jax.random.split(key, 12)
        s2 = 1.0 / np.sqrt(2 * D)
        s1 = 1.0 / np.sqrt(D)
        return {'input': jax.random.normal(ks[0], (B, N, D), jnp.float32), 'in_matrix': jax.random.uniform(ks[1], (N, N), jnp.float32), 'out_matrix': jax.random.uniform(ks[2], (N, N), jnp.float32), 'w3_w': jax.random.normal(ks[3], (D, 2 * D), jnp.float32) * s2, 'w3_b': jnp.zeros((D,), jnp.float32), 'u3_w': jax.random.normal(ks[4], (D, D), jnp.float32) * s1, 'u3_b': jnp.zeros((D,), jnp.float32), 'w4_w': jax.random.normal(ks[5], (D, 2 * D), jnp.float32) * s2, 'w4_b': jnp.zeros((D,), jnp.float32), 'w5_w': jax.random.normal(ks[6], (D, 2 * D), jnp.float32) * s2, 'w5_b': jnp.zeros((D,), jnp.float32), 'u5_w': jax.random.normal(ks[7], (D, D), jnp.float32) * s1, 'u5_b': jnp.zeros((D,), jnp.float32), 'time_step': TIME_STEP}
    _L0_gnn_all = _L0_gnn_setup()
    _L0_gnn_in = {k: v for k, v in _L0_gnn_all.items() if k in ('w3_w', 'w3_b', 'u3_w', 'u3_b', 'w4_w', 'w4_b', 'w5_w', 'w5_b', 'u5_w', 'u5_b')}
    del _L0_gnn_all

    def _L1_gnn_setup():
        import jax, jax.numpy as jnp
        import numpy as np
        B, N, F_IN, F_OUT, ORDERS = (32, 1024, 128, 128, 2)
        NUM_MATRICES = 2 * ORDERS + 1

        def _cheb_hops(x0, A, orders):
            hops = []
            x1 = jnp.einsum('bnf,nw->bwf', x0, A)
            hops.append(x1)
            xk_1, xk_2 = (x1, x0)
            for _ in range(2, orders + 1):
                x2 = 2.0 * jnp.einsum('bnf,nw->bwf', xk_1, A) - xk_2
                hops.append(x2)
                xk_1, xk_2 = (x2, xk_1)
            return hops
        key = jax.random.key(seed)
        k1, k2, k3, k4, k5 = jax.random.split(key, 5)
        X = jax.random.normal(k1, (B, N, F_IN), dtype=jnp.float32)
        A1 = jax.random.uniform(k2, (N, N), dtype=jnp.float32) * (2.0 / N)
        A2 = jax.random.uniform(k3, (N, N), dtype=jnp.float32) * (2.0 / N)
        stdv = 1.0 / np.sqrt(F_OUT)
        Theta1 = jax.random.uniform(k4, (F_IN * NUM_MATRICES, F_OUT), dtype=jnp.float32, minval=-stdv, maxval=stdv)
        bias = jax.random.uniform(k5, (F_OUT,), dtype=jnp.float32, minval=-stdv, maxval=stdv)
        return {'X': X, 'A1': A1, 'A2': A2, 'Theta1': Theta1, 'bias': bias}
    _L1_gnn_all = _L1_gnn_setup()
    _L1_gnn_in = {k: v for k, v in _L1_gnn_all.items() if k in ('Theta1', 'bias')}
    del _L1_gnn_all

    def _L2_gnn_setup():
        import jax, jax.numpy as jnp
        import numpy as np
        B, N, D = (4, 4096, 128)
        key = jax.random.key(seed)
        kx, ka, kq, kk, kv = jax.random.split(key, 5)
        x = jax.random.normal(kx, (B, N, D), dtype=jnp.float32)
        mask = (jax.random.uniform(ka, (N, N)) < 0.05).astype(jnp.float32)
        A_shape = jnp.clip(mask + jnp.eye(N, dtype=jnp.float32), 0.0, 1.0)
        q = jax.random.normal(kq, (D, D), dtype=jnp.float32)
        k = jax.random.normal(kk, (D, D), dtype=jnp.float32)
        v = jax.random.normal(kv, (D, D), dtype=jnp.float32)
        return {'x': x, 'A_shape': A_shape, 'q': q, 'k': k, 'v': v}
    _L2_gnn_all = _L2_gnn_setup()
    _L2_gnn_in = {k: v for k, v in _L2_gnn_all.items() if k in ('q', 'k', 'v')}
    del _L2_gnn_all

    def _L3_gnn_setup():
        import jax, jax.numpy as jnp
        import numpy as np
        B, N, F_IN, F_OUT, K = (16, 1024, 128, 128, 3)

        def _scaled_laplacian(adj):
            n = adj.shape[0]
            A = adj * (1.0 - jnp.eye(n, dtype=adj.dtype))
            deg = A.sum(axis=1)
            safe = jnp.where(deg > 0, deg, 1.0)
            dinv = jnp.where(deg > 0, 1.0 / jnp.sqrt(safe), 0.0)
            return -(dinv[:, None] * A * dinv[None, :])
        key = jax.random.key(seed)
        k1, k2, k3, _ = jax.random.split(key, 4)
        x = jax.random.normal(k1, (B, N, F_IN), dtype=jnp.float32)
        adj = jax.random.uniform(k2, (N, N), dtype=jnp.float32)
        Ws = jax.random.normal(k3, (K, F_IN, F_OUT), dtype=jnp.float32) / np.float32(np.sqrt(F_IN))
        bias = jnp.zeros((F_OUT,), dtype=jnp.float32)
        return {'x': x, 'adj': adj, 'Ws': Ws, 'bias': bias}
    _L3_gnn_all = _L3_gnn_setup()
    _L3_gnn_in = {k: v for k, v in _L3_gnn_all.items() if k in ('Ws', 'bias')}
    del _L3_gnn_all
    return {'x': x, 'adj': adj, 'L0_gnn_w3_w': _L0_gnn_in['w3_w'], 'L0_gnn_w3_b': _L0_gnn_in['w3_b'], 'L0_gnn_u3_w': _L0_gnn_in['u3_w'], 'L0_gnn_u3_b': _L0_gnn_in['u3_b'], 'L0_gnn_w4_w': _L0_gnn_in['w4_w'], 'L0_gnn_w4_b': _L0_gnn_in['w4_b'], 'L0_gnn_w5_w': _L0_gnn_in['w5_w'], 'L0_gnn_w5_b': _L0_gnn_in['w5_b'], 'L0_gnn_u5_w': _L0_gnn_in['u5_w'], 'L0_gnn_u5_b': _L0_gnn_in['u5_b'], 'L1_gnn_Theta1': _L1_gnn_in['Theta1'], 'L1_gnn_bias': _L1_gnn_in['bias'], 'L2_gnn_q': _L2_gnn_in['q'], 'L2_gnn_k': _L2_gnn_in['k'], 'L2_gnn_v': _L2_gnn_in['v'], 'L3_gnn_Ws': _L3_gnn_in['Ws'], 'L3_gnn_bias': _L3_gnn_in['bias']}

def reference(x, adj, L0_gnn_w3_w, L0_gnn_w3_b, L0_gnn_u3_w, L0_gnn_u3_b, L0_gnn_w4_w, L0_gnn_w4_b, L0_gnn_w5_w, L0_gnn_w5_b, L0_gnn_u5_w, L0_gnn_u5_b, L1_gnn_Theta1, L1_gnn_bias, L2_gnn_q, L2_gnn_k, L2_gnn_v, L3_gnn_Ws, L3_gnn_bias):
    import jax
    import jax.numpy as jnp

    def _L0_gnn_ref(input, in_matrix, out_matrix, w3_w, w3_b, u3_w, u3_b, w4_w, w4_b, w5_w, w5_b, u5_w, u5_b, time_step):
        import jax, jax.numpy as jnp
        import numpy as np
        B, N, D = (32, 512, 128)
        TIME_STEP = 5

        def step(h, _):
            m_in = jnp.einsum('nm,bmd->bnd', in_matrix, h)
            m_out = jnp.einsum('nm,bmd->bnd', out_matrix, h)
            av = jnp.concatenate([m_in, m_out], axis=-1)
            u3 = h @ u3_w.T + u3_b
            z = jax.nn.sigmoid(av @ w3_w.T + w3_b + u3)
            r = jax.nn.sigmoid(av @ w4_w.T + w4_b + u3)
            hv = jnp.tanh(av @ w5_w.T + w5_b + (r * h @ u5_w.T + u5_b))
            h = (1.0 - z) * h + z * hv
            return (h, None)
        h, _ = jax.lax.scan(step, input, None, length=time_step)
        return h

    def _L1_gnn_ref(X, A1, A2, Theta1, bias):
        import jax, jax.numpy as jnp
        import numpy as np
        B, N, F_IN, F_OUT, ORDERS = (32, 1024, 128, 128, 2)
        NUM_MATRICES = 2 * ORDERS + 1

        def _cheb_hops(x0, A, orders):
            hops = []
            x1 = jnp.einsum('bnf,nw->bwf', x0, A)
            hops.append(x1)
            xk_1, xk_2 = (x1, x0)
            for _ in range(2, orders + 1):
                x2 = 2.0 * jnp.einsum('bnf,nw->bwf', xk_1, A) - xk_2
                hops.append(x2)
                xk_1, xk_2 = (x2, xk_1)
            return hops
        xs = [X] + _cheb_hops(X, A1, ORDERS) + _cheb_hops(X, A2, ORDERS)
        x = jnp.stack(xs, axis=2)
        b, n = (X.shape[0], X.shape[1])
        x = x.reshape(b, n, -1)
        out = jax.nn.relu(x @ Theta1 + bias)
        return out

    def _L2_gnn_ref(x, A_shape, q, k, v):
        import jax, jax.numpy as jnp
        import numpy as np
        B, N, D = (4, 4096, 128)
        input_dimension = x.shape[-1]
        Q = x @ q
        K = x @ k
        A = jnp.einsum('bnd,bmd->bnm', Q, K)
        A = A / jnp.sqrt(jnp.float32(input_dimension))
        A = jnp.tanh(A / 8.0) * 8.0
        A = jnp.exp(A) * A_shape
        A = A / jnp.sum(A, axis=-1, keepdims=True)
        out = A @ x @ v
        return out

    def _L3_gnn_ref(x, adj, Ws, bias):
        import jax, jax.numpy as jnp
        import numpy as np
        B, N, F_IN, F_OUT, K = (16, 1024, 128, 128, 3)

        def _scaled_laplacian(adj):
            n = adj.shape[0]
            A = adj * (1.0 - jnp.eye(n, dtype=adj.dtype))
            deg = A.sum(axis=1)
            safe = jnp.where(deg > 0, deg, 1.0)
            dinv = jnp.where(deg > 0, 1.0 / jnp.sqrt(safe), 0.0)
            return -(dinv[:, None] * A * dinv[None, :])
        L = _scaled_laplacian(adj)
        Tx0 = x
        out = jnp.einsum('bnf,fo->bno', Tx0, Ws[0])
        Tx1 = jnp.einsum('mn,bnf->bmf', L, Tx0)
        out = out + jnp.einsum('bnf,fo->bno', Tx1, Ws[1])
        for k in range(2, K):
            Tx2 = 2.0 * jnp.einsum('mn,bnf->bmf', L, Tx1) - Tx0
            out = out + jnp.einsum('bnf,fo->bno', Tx2, Ws[k])
            Tx0, Tx1 = (Tx1, Tx2)
        return out + bias
    x = _layernorm(x + _L0_gnn_ref(x, adj, adj, L0_gnn_w3_w, L0_gnn_w3_b, L0_gnn_u3_w, L0_gnn_u3_b, L0_gnn_w4_w, L0_gnn_w4_b, L0_gnn_w5_w, L0_gnn_w5_b, L0_gnn_u5_w, L0_gnn_u5_b, 5), axis=-1)
    x = _layernorm(x + _L1_gnn_ref(x, adj, adj, L1_gnn_Theta1, L1_gnn_bias), axis=-1)
    x = _layernorm(x + _L2_gnn_ref(x, adj, L2_gnn_q, L2_gnn_k, L2_gnn_v), axis=-1)
    x = _layernorm(x + _L3_gnn_ref(x, adj, L3_gnn_Ws, L3_gnn_bias), axis=-1)
    return x

_drawn_inputs = setup_inputs


def setup_inputs(seed=0):
    import zlib

    import numpy as np

    out = dict(_drawn_inputs(seed))
    spreads = {'L0_gnn_w3_b': (0.0, 0.1),
     'L0_gnn_u3_b': (0.0, 0.1),
     'L0_gnn_w4_b': (0.0, 0.356),
     'L0_gnn_w5_b': (0.0, 0.1),
     'L0_gnn_u5_b': (0.0, 0.1),
     'L3_gnn_bias': (0.0, 0.1)}
    factors = {'L1_gnn_bias': 2.961}
    for name, (base, spread) in spreads.items():
        noise = np.random.default_rng([zlib.crc32(name.encode()), seed]).standard_normal(out[name].shape)
        drawn = base * np.exp(spread * noise) if base else spread * noise
        out[name] = jnp.asarray(drawn.astype(out[name].dtype))
    for name, factor in factors.items():
        out[name] = (out[name] * factor).astype(out[name].dtype)
    return out
```

```python
from contextlib import ExitStack

import concourse.bass as bass
from concourse import mybir

F32 = mybir.dt.float32
F32R = mybir.dt.float32r
ALU = mybir.AluOpType
ACT = mybir.ActivationFunctionType
AX_X = mybir.AxisListType.X

P = 128
LANES = 4
STEPS = 5
EPS = 1e-5

STAGES = [("X0", 0)]
for step in range(STEPS):
    STAGES += [("A", 0), ("R", 0), ("U", 0), ("T", 0) if step < STEPS - 1 else ("TL", 0)]
STAGES += [("XA", 1), ("Y", 1), ("YT", 1), ("Z", 1), ("ZT", 1)]
STAGES += [("X2", 2), ("G", 2), ("S", 0), ("S", 1), ("S", 2), ("S", 3), ("O", 2), ("V", 2), ("VT", 2)]
STAGES += [("XA", 3), ("Y", 3), ("YT", 3), ("Z", 3), ("ZT", 3)]
J = len(STAGES)
NORMS = [("TL", 0), ("ZT", 1), ("VT", 2), ("ZT", 3)]

GIVEN = {
    "bank0": ["X0", "R", "U", "T", "TL", "XA", "Y", "YT", "ZT", "X2", "S", "O", "VT"],
    "bank1": ["A", "U", "XA", "Z", "G", "O", "V"],
    "m_hi": ["A", "XA", "S", "O"],
    "t_hi": ["X0", "T", "XA", "X2"],
    "n_hi": ["X0", "T", "TL", "YT", ("ZT", 1), "VT"],
    "q_hi": ["R", "G"],
    "r_tanh": ["R", "S"],
    "s_exp": ["S"],
    "z_tanh": ["U"],
    "v_tanh": ["U"],
    "hT_copied": ["X0", "Y", "Z", "V"],
    "m_lo": ["A", "XA", "S", "O"],
    "t_lo": ["X0", "T", "XA", "X2"],
    "n_lo": ["X0", "T", "TL", "YT", ("ZT", 1), "VT"],
    "q_lo": ["R", "G"],
    "rh": ["R"],
    "v_minus_h": ["U"],
    "z_scaled": ["U"],
    "h_new": ["U"],
    "masked": ["S"],
    "recip": ["O"],
    "summed": NORMS,
    "stats": NORMS,
    "moments": NORMS,
    "normed": NORMS,
    "var_eps": NORMS,
    "rstd": NORMS,
    "e_sum": ["S"],
}


def given(signal, j):
    return sum(1 for s in STAGES[:max(j + 1, 0)] if s in GIVEN[signal] or s[0] in GIVEN[signal])


def back(slot, lane, lag):
    n = slot * LANES + lane - lag
    return n // LANES, n % LANES


class At:

    def __init__(self, j, g, i):
        self.j, self.g, self.i = j, g, i

    def upto(self, signal, j):
        n = given(signal, j) + self.g * given(signal, J - 1)
        if self.i is not None:
            n = n + self.i * (given(signal, 8) - given(signal, 4))
        return n

    def now(self, signal):
        return self.upto(signal, self.j)

    def before(self, signal):
        return self.upto(signal, self.j - 1)


def turns(first, last, g, i, lags, emit):
    for slot in range(first, last):
        for lane in range(LANES):
            for part in lags:
                s, k = back(slot, lane, part)
                if 0 <= s - k < J:
                    kind, layer = STAGES[s - k]
                    emit(kind, layer, part, k, At(s - k, g, i))


def schedule(engine, groups, lags, emit):
    with engine.Fori(0, groups) as g:
        turns(0, 5, g, None, lags, emit)
        with engine.Fori(0, STEPS - 2) as i:
            turns(5, 9, g, i, lags, emit)
        turns(5 + 4 * (STEPS - 2), J + LANES, g, None, lags, emit)


def resnorm_gnn(nc, x, adj, w3_w, w3_b, u3_w, u3_b, w4_w, w4_b, w5_w, w5_b, u5_w, u5_b,
                theta, bias1, q_w, k_w, v_w, ws, bias3, out):
    B, N, D = x.shape
    assert D == P and N % P == 0 and B % LANES == 0
    C = N // P
    GROUPS = B // LANES
    SCORE = 1.0 / (8.0 * float(D) ** 0.5)

    with ExitStack() as ctx:
        def sb(name, shape, dt=F32):
            return ctx.enter_context(nc.sbuf_tensor(name, shape, dt))

        def sem(name):
            return ctx.enter_context(nc.semaphore(name))

        def lanes(name, shape, dt=F32):
            return [sb(f"{name}{k}", shape, dt) for k in range(LANES)]

        At_f = sb("At_f", [P, C, N])
        adj_hi, adj_lo = sb("adj_hi", [P, C, N], F32R), sb("adj_lo", [P, C, N], F32R)
        adjT_hi, adjT_lo = sb("adjT_hi", [P, C, N], F32R), sb("adjT_lo", [P, C, N], F32R)
        lapT_hi, lapT_lo = sb("lapT_hi", [P, C, N], F32R), sb("lapT_lo", [P, C, N], F32R)
        ONES_W, W4, W34, W5, U3, U5H, T0, T1, T2, QK, VV, L0, L1, L2 = range(-1, 13)
        NW = 13
        w_hi, w_lo = sb("w_hi", [P, NW, P], F32R), sb("w_lo", [P, NW, P], F32R)
        ident = sb("ident", [P, P])
        ones = sb("ones", [P, P])
        cols = sb("cols", [P, 16])
        bias = sb("bias", [P, 4])
        BR, BZ, BV = range(3)
        neg_half = sb("neg_half", [P, C])
        eps = sb("eps", [P, C])
        zeros = sb("zeros", [P, N])
        deg = sb("deg", [P, 6, C])

        x_in = lanes("x_in", [P, C, P])
        x_nat = lanes("x_nat", [P, C, P])
        n_hi, n_lo = lanes("n_hi", [P, C, P], F32R), lanes("n_lo", [P, C, P], F32R)
        hT = lanes("hT", [P, N])
        t_hi, t_lo = lanes("t_hi", [P, N], F32R), lanes("t_lo", [P, N], F32R)
        m_hi, m_lo = lanes("m_hi", [P, N], F32R), lanes("m_lo", [P, N], F32R)
        q_hi, q_lo = lanes("q_hi", [P, N], F32R), lanes("q_lo", [P, N], F32R)
        r_buf, z_buf, v_buf = lanes("r_buf", [P, N]), lanes("z_buf", [P, N]), lanes("v_buf", [P, N])
        stats = lanes("stats", [P, C, 6])
        moments = lanes("moments", [P, C, 2])
        rstd = lanes("rstd", [P, 2, C])
        recip = lanes("recip", [P, C])

        bank0 = [ctx.enter_context(nc.psum_tensor(f"bank0_{k}", [P, N], F32)) for k in range(LANES)]
        bank1 = [ctx.enter_context(nc.psum_tensor(f"bank1_{k}", [P, N], F32)) for k in range(LANES)]

        sig = {s: [sem(f"{s}_{k}") for k in range(LANES)] for s in GIVEN}
        loaded = [sem(f"loaded_{k}") for k in range(LANES)]
        x_nat_free = [sem(f"x_nat_free_{k}") for k in range(LANES)]
        adj_loaded = sem("adj_loaded")
        w_loaded = sem("w_loaded")
        s_const = sem("s_const")
        s_ones = sem("s_ones")
        s_pe = sem("s_pe")
        s_dve = sem("s_dve")
        s_act = sem("s_act")
        s_pool = sem("s_pool")

        A_f = [r_buf[c] for c in range(C)]
        B_f = [z_buf[c] for c in range(C)]
        wraw = [x_nat[k] for k in range(LANES)]
        wsum = v_buf

        adj_rows = adj.rearrange("(c p) n -> p c n", p=P)
        x_rows = x.rearrange("b (c p) d -> b p c d", p=P)
        out_rows = out.rearrange("b (c p) d -> b p c d", p=P)

        block = ctx.enter_context(nc.Block())

        def raw(i):
            return wraw[i // C][:, i % C, :]
        R_W3A, R_W3B, R_W4A, R_W4B, R_W5A, R_W5B, R_U3, R_U5, R_Q, R_K = range(10)
        R_TH = 10
        ws_raw = hT[0]
        v_raw = hT[1]

        @block.sync
        def _(sp):
            for c in range(C):
                sp.dma_start(A_f[c][:], adj_rows[:, c, :]).then_inc(adj_loaded, 16)
            for dst, src in [(R_W3A, w3_w[:, 0:P]), (R_W3B, w3_w[:, P:2 * P]), (R_W4A, w4_w[:, 0:P]),
                             (R_W4B, w4_w[:, P:2 * P]), (R_W5A, w5_w[:, 0:P]), (R_W5B, w5_w[:, P:2 * P]),
                             (R_U3, u3_w), (R_U5, u5_w), (R_Q, q_w), (R_K, k_w)]:
                sp.dma_start(raw(dst), src).then_inc(w_loaded, 16)
            for t in range(5):
                sp.dma_start(raw(R_TH + t), theta[t * P:(t + 1) * P, :]).then_inc(w_loaded, 16)
            sp.dma_start(ws_raw[:, 0:3 * P].rearrange("p (k o) -> p k o", k=3),
                         ws.rearrange("k f o -> f k o")).then_inc(w_loaded, 16)
            sp.dma_start(v_raw[:, 0:P], v_w).then_inc(w_loaded, 16)
            for n, b in enumerate([w3_b, w4_b, w5_b, u3_b, u5_b, bias1, bias3]):
                sp.dma_start(cols[:, n:n + 1], b.rearrange("(p a) -> p a", a=1)).then_inc(w_loaded, 16)
            for k in range(LANES):
                sp.dma_start(x_in[k][:], x_rows[k]).then_inc(loaded[k], 16)
            with sp.Fori(0, GROUPS - 1) as g:
                for k in range(LANES):
                    sp.wait_ge(sig["summed"][k], g * len(NORMS) + 1)
                    src = x_rows[bass.ds(g * LANES + (k + LANES), 1)].rearrange("a p c d -> (a p) c d")
                    sp.dma_start(x_in[k][:], src).then_inc(loaded[k], 16)
                for k in range(LANES):
                    sp.wait_ge(sig["normed"][k], g * len(NORMS) + len(NORMS))
                    dst = out_rows[bass.ds(g * LANES + k, 1)].rearrange("a p c d -> (a p) c d")
                    sp.dma_start(dst, x_nat[k][:]).then_inc(x_nat_free[k], 16)
            for k in range(LANES):
                sp.wait_ge(sig["normed"][k], GROUPS * len(NORMS))
                sp.dma_start(out_rows[B - LANES + k], x_nat[k][:]).then_inc(x_nat_free[k], 16)
            for k in range(LANES):
                sp.wait_ge(x_nat_free[k], 16 * GROUPS + 1)

        W_ALL = 16 * (10 + 5 + 2 + 7)

        @block.tensor
        def _(pe):
            def three(dst, st_hi, st_lo, mv_hi, mv_lo, start, stop):
                pe.matmul(dst, st_hi, mv_hi, start=start, stop=False)
                pe.matmul(dst, st_hi, mv_lo, start=False, stop=False)
                return pe.matmul(dst, st_lo, mv_hi, start=False, stop=stop)

            pe.wait_ge(s_const, 1)
            pe.wait_ge(adj_loaded, 16 * C)
            for c in range(C):
                for r in range(C):
                    mm = pe.transpose(bank0[c][:, r * P:(r + 1) * P], A_f[r][:, c * P:(c + 1) * P], ident[:])
                mm.then_inc(s_pe, 1)
            pe.wait_ge(w_loaded, W_ALL)
            pe.wait_ge(s_dve, 2)
            for n, src in enumerate([wsum[0][:, 0:P], wsum[0][:, P:2 * P], wsum[0][:, 2 * P:3 * P], raw(R_U3)]):
                mm = pe.transpose(bank1[0][:, n * P:(n + 1) * P], src, ident[:])
            mm.then_inc(s_pe, 1)
            for n, src in enumerate([raw(R_U5), raw(R_Q), raw(R_K)]):
                mm = pe.transpose(bank1[1][:, n * P:(n + 1) * P], src, ident[:])
            mm.then_inc(s_pe, 1)
            pe.wait_ge(s_dve, 3)
            pe.matmul(bank1[2][:, 0:P], wsum[1][:, 0:P], wsum[1][:, P:2 * P], start=True, stop=True).then_inc(s_pe, 1)
            pe.wait_ge(s_dve, 4)
            pe.wait_ge(s_act, 1)
            for c in range(C):
                for r in range(C):
                    mm = pe.transpose(bank0[c][:, r * P:(r + 1) * P], B_f[r][:, c * P:(c + 1) * P], ident[:])
                mm.then_inc(s_pe, 1)
            pe.wait_ge(s_dve, 4 + C)
            pe.wait_ge(s_act, 2)

            def emit(kind, layer, part, k, at):
                def need(signal):
                    pe.wait_ge(sig[signal][k], at.before(signal))

                b0, b1 = bank0[k][:], bank1[k][:]

                def transposes(src):
                    for c in range(C):
                        mm = pe.transpose(bank0[k][:, c * P:(c + 1) * P], src(c), ident[:])
                    mm.then_inc(sig["bank0"][k], 1)

                def over_rows(dst, mv_hi, mv_lo, start):
                    need("n_hi")
                    for c in range(C):
                        pe.matmul(dst, n_hi[k][:, c, :], mv_hi[:, c, :], start=start and c == 0, stop=False)
                        pe.matmul(dst, n_hi[k][:, c, :], mv_lo[:, c, :], start=False, stop=False)
                    need("n_lo")
                    for c in range(C):
                        mm = pe.matmul(dst, n_lo[k][:, c, :], mv_hi[:, c, :], start=False, stop=(c == C - 1))
                    return mm

                def weight(dst, w, mv_hi, mv_lo, start, stop):
                    return three(dst, w_hi[:, w, :], w_lo[:, w, :], mv_hi[k][:], mv_lo[k][:], start, stop)

                if kind == "X0":
                    pe.wait_ge(loaded[k], at.g * 16 + 16)
                    transposes(lambda c: x_in[k][:, c, :])
                elif kind == "A":
                    over_rows(b1, adjT_hi, adjT_lo, True).then_inc(sig["bank1"][k], 1)
                elif kind == "R":
                    need("t_hi")
                    need("t_lo")
                    weight(b0, U3, t_hi, t_lo, True, False)
                    need("m_hi")
                    need("m_lo")
                    weight(b0, W4, m_hi, m_lo, False, True).then_inc(sig["bank0"][k], 1)
                    weight(b1, W5, m_hi, m_lo, True, False)
                elif kind == "U":
                    need("r_tanh")
                    pe.matmul(b0, w_hi[:, W34, :], m_hi[k][:], start=False, stop=False, skip_group_check=True)
                    pe.matmul(b0, w_hi[:, W34, :], m_lo[k][:], start=False, stop=False, skip_group_check=True)
                    pe.matmul(b0, w_lo[:, W34, :], m_hi[k][:], start=False, stop=True, skip_group_check=True)\
                        .then_inc(sig["bank0"][k], 1)
                    need("q_hi")
                    need("q_lo")
                    weight(b1, U5H, q_hi, q_lo, False, True).then_inc(sig["bank1"][k], 1)
                elif kind in ("T", "TL"):
                    need("h_new")
                    transposes(lambda c: hT[k][:, c * P:(c + 1) * P])
                elif kind == "XA":
                    mv_hi, mv_lo = (adj_hi, adj_lo) if layer == 1 else (lapT_hi, lapT_lo)
                    need("normed")
                    transposes(lambda c: x_nat[k][:, c, :])
                    over_rows(b1, mv_hi, mv_lo, True).then_inc(sig["bank1"][k], 1)
                elif kind == "Y":
                    need("t_hi")
                    need("t_lo")
                    weight(b0, T1 if layer == 1 else L1, t_hi, t_lo, True, False)
                    need("m_hi")
                    need("m_lo")
                    weight(b0, T2 if layer == 1 else L2, m_hi, m_lo, False, True).then_inc(sig["bank0"][k], 1)
                elif kind == "YT":
                    need("hT_copied")
                    transposes(lambda c: hT[k][:, c * P:(c + 1) * P])
                    weight(b1, T0 if layer == 1 else L0, t_hi, t_lo, True, False)
                elif kind == "Z":
                    mv_hi, mv_lo = (adj_hi, adj_lo) if layer == 1 else (lapT_hi, lapT_lo)
                    over_rows(b1, mv_hi, mv_lo, False).then_inc(sig["bank1"][k], 1)
                elif kind in ("ZT", "VT"):
                    need("hT_copied")
                    transposes(lambda c: hT[k][:, c * P:(c + 1) * P])
                elif kind == "X2":
                    need("normed")
                    transposes(lambda c: x_nat[k][:, c, :])
                elif kind == "G":
                    need("t_hi")
                    need("t_lo")
                    weight(b1, QK, t_hi, t_lo, True, True).then_inc(sig["bank1"][k], 1)
                if kind in ("S", "O"):
                    c = layer if kind == "S" else C
                    if c > 0:
                        need("m_hi")
                        if c == 1:
                            need("n_hi")
                            need("n_lo")
                        pe.matmul(b1, n_hi[k][:, c - 1, :], m_hi[k][:], start=(c == 1), stop=False)
                        pe.matmul(b1, n_lo[k][:, c - 1, :], m_hi[k][:], start=False, stop=False)
                        need("m_lo")
                        mm = pe.matmul(b1, n_hi[k][:, c - 1, :], m_lo[k][:], start=False, stop=(c == C))
                        if c == C:
                            mm.then_inc(sig["bank1"][k], 1)
                    if c < C:
                        if c == 0:
                            need("q_hi")
                            need("q_lo")
                        s = slice(c * P, (c + 1) * P)
                        three(b0, t_hi[k][:, s], t_lo[k][:, s], q_hi[k][:], q_lo[k][:], True, True)\
                            .then_inc(sig["bank0"][k], 1)
                    else:
                        need("e_sum")
                        for r in range(C):
                            mm = pe.matmul(bank0[k][:, 2 * r:2 * r + 2], v_buf[k][:, r * P:(r + 1) * P],
                                           ones[:, 0:2], start=True, stop=True)
                        mm.then_inc(sig["bank0"][k], 1)
                if kind == "V":
                    need("m_hi")
                    need("m_lo")
                    weight(b1, VV, m_hi, m_lo, True, True).then_inc(sig["bank1"][k], 1)

            schedule(pe, GROUPS, (0,), emit)

        @block.scalar
        def _(act):
            act.wait_ge(adj_loaded, 16 * C)
            for c in range(C):
                act.activation(adj_hi[:, c, :], A_f[c][:], ACT.Copy)
            for c in range(C):
                act.wait_ge(s_pe, c + 1)
                act.activation(At_f[:, c, :], bank0[c][:], ACT.Copy)
                mm = act.activation(adjT_hi[:, c, :], bank0[c][:], ACT.Copy)
            mm.then_inc(s_act, 1)
            act.wait_ge(s_dve, 4)
            for c in range(C):
                act.wait_ge(s_pe, 7 + c + 1)
                mm = act.activation(lapT_hi[:, c, :], bank0[c][:], ACT.Copy, scale=deg[:, 5, c:c + 1])
                mm.then_inc(s_pool, 1)
            act.wait_ge(s_dve, 4)
            act.activation(cols[:, 8:9], cols[:, 0:1], ACT.Exp).then_inc(s_act, 1)

            def emit(kind, layer, part, k, at):
                def wait(signal):
                    act.wait_ge(sig[signal][k], at.now(signal))

                def copy(signal, dst, src):
                    act.activation(dst, src, ACT.Copy).then_inc(sig[signal][k], 1)

                b0, b1 = bank0[k][:], bank1[k][:]
                key = (kind, part)
                if key == ("X0", 0):
                    act.wait_ge(loaded[k], at.g * 16 + 16)
                    copy("n_hi", n_hi[k][:], x_in[k][:])
                    wait("bank0")
                    copy("hT_copied", hT[k][:], b0)
                    copy("t_hi", t_hi[k][:], b0)
                elif key == ("A", 0):
                    wait("bank1")
                    copy("m_hi", m_hi[k][:], b1)
                elif key == ("R", 0):
                    wait("bank0")
                    act.activation(r_buf[k][:], b0, ACT.Tanh, bias=bias[:, BR:BR + 1], scale=0.5)\
                        .then_inc(sig["r_tanh"][k], 1)
                elif key == ("R", 1):
                    wait("rh")
                    copy("q_hi", q_hi[k][:], r_buf[k][:])
                elif key == ("U", 0):
                    wait("bank0")
                    act.activation(z_buf[k][:], b0, ACT.Tanh, bias=bias[:, BZ:BZ + 1], scale=0.5)\
                        .then_inc(sig["z_tanh"][k], 1)
                    wait("bank1")
                    act.activation(v_buf[k][:], b1, ACT.Tanh, bias=bias[:, BV:BV + 1]).then_inc(sig["v_tanh"][k], 1)
                elif key == ("T", 0):
                    wait("bank0")
                    copy("n_hi", n_hi[k][:], b0)
                    copy("t_hi", t_hi[k][:], hT[k][:])
                elif kind in ("TL", "ZT", "VT") and part == 2 and layer < 3:
                    wait("normed")
                    copy("n_hi", n_hi[k][:], x_nat[k][:])
                elif key == ("XA", 0):
                    wait("bank0")
                    copy("t_hi", t_hi[k][:], b0)
                    wait("bank1")
                    copy("m_hi", m_hi[k][:], b1)
                elif key == ("X2", 0):
                    wait("bank0")
                    copy("t_hi", t_hi[k][:], b0)
                elif key == ("Y", 0):
                    wait("bank0")
                    copy("hT_copied", hT[k][:], b0)
                elif key == ("YT", 0):
                    wait("bank0")
                    copy("n_hi", n_hi[k][:], b0)
                elif key == ("Z", 0):
                    wait("bank1")
                    act.activation(hT[k][:], b1, ACT.Relu if layer == 1 else ACT.Identity,
                                   bias=cols[:, 5:6] if layer == 1 else cols[:, 6:7])\
                        .then_inc(sig["hT_copied"][k], 1)
                elif key == ("G", 0):
                    wait("bank1")
                    copy("q_hi", q_hi[k][:], b1)
                elif key == ("S", 0):
                    if layer > 0:
                        act.wait_ge(sig["e_sum"][k], at.before("e_sum"))
                    wait("bank0")
                    act.activation(r_buf[k][:], b0, ACT.Tanh, scale=SCORE).then_inc(sig["r_tanh"][k], 1)
                    wait("r_tanh")
                    act.activation(r_buf[k][:], r_buf[k][:], ACT.Exp, scale=8.0).then_inc(sig["s_exp"][k], 1)
                elif key == ("S", 1):
                    wait("masked")
                    copy("m_hi", m_hi[k][:], r_buf[k][:])
                elif key == ("O", 0):
                    wait("bank1")
                    copy("m_hi", m_hi[k][:], b1)
                elif key == ("V", 0):
                    wait("bank1")
                    copy("hT_copied", hT[k][:], b1)

            schedule(act, GROUPS, (0, 1, 2), emit)

        @block.vector
        def _(dve):
            own = sem("own_dve")
            n_own = [0]

            def step(ins):
                n_own[0] += 1
                ins.then_inc(own, 1)

            def fence():
                dve.wait_ge(own, n_own[0])

            dve.memset(ones[:], 1.0).then_inc(s_ones, 1)
            dve.memset(eps[:], EPS)
            dve.memset(zeros[:], 0.0)
            dve.memset(neg_half[:], -0.5).then_inc(s_dve, 1)
            dve.wait_ge(w_loaded, W_ALL)
            step(dve.tensor_tensor(wsum[0][:, 0:P], raw(R_W4A), raw(R_W4B), ALU.add))
            step(dve.tensor_tensor(wsum[0][:, 3 * P:4 * P], raw(R_W3A), raw(R_W3B), ALU.add))
            fence()
            step(dve.tensor_tensor(wsum[0][:, P:2 * P], wsum[0][:, 3 * P:4 * P], wsum[0][:, 0:P], ALU.subtract))
            fence()
            dve.tensor_tensor(wsum[0][:, 2 * P:3 * P], raw(R_W5A), raw(R_W5B), ALU.add).then_inc(s_dve, 1)
            wf = [hT[2][:, 0:P], hT[2][:, P:2 * P], hT[2][:, 2 * P:3 * P], hT[2][:, 3 * P:4 * P],
                  hT[3][:, 0:P], hT[3][:, P:2 * P], hT[3][:, 2 * P:3 * P], hT[3][:, 3 * P:4 * P],
                  wsum[2][:, 0:P], wsum[2][:, P:2 * P], wsum[2][:, 2 * P:3 * P], wsum[2][:, 3 * P:4 * P],
                  wsum[3][:, 0:P]]
            tmp = wsum[3][:, P:2 * P]
            step(dve.tensor_tensor(tmp, raw(R_TH + 2), raw(R_TH + 4), ALU.add))
            fence()
            step(dve.tensor_tensor(wf[T0], raw(R_TH), tmp, ALU.subtract))
            step(dve.tensor_scalar(wf[T2], tmp, 2.0, None, ALU.mult))
            step(dve.tensor_tensor(wf[T1], raw(R_TH + 1), raw(R_TH + 3), ALU.add))
            step(dve.tensor_tensor(wf[L0], ws_raw[:, 0:P], ws_raw[:, 2 * P:3 * P], ALU.subtract))
            step(dve.tensor_copy(wf[L1], ws_raw[:, P:2 * P]))
            step(dve.tensor_scalar(wf[L2], ws_raw[:, 2 * P:3 * P], 2.0, None, ALU.mult))
            step(dve.tensor_copy(wf[VV], v_raw[:, 0:P]))
            step(dve.tensor_tensor(cols[:, 9:10], cols[:, 1:2], cols[:, 3:4], ALU.add))
            step(dve.tensor_tensor(cols[:, 10:11], cols[:, 0:1], cols[:, 3:4], ALU.add))
            step(dve.tensor_tensor(bias[:, BV:BV + 1], cols[:, 2:3], cols[:, 4:5], ALU.add))
            fence()
            step(dve.tensor_scalar(bias[:, BR:BR + 1], cols[:, 9:10], 0.5, None, ALU.mult))
            step(dve.tensor_scalar(bias[:, BZ:BZ + 1], cols[:, 10:11], 0.5, None, ALU.mult))
            dve.wait_ge(s_pe, C + 2)
            dve.tensor_copy(wsum[1][:, 0:2 * P], bank1[1][:, P:3 * P]).then_inc(s_dve, 1)
            for w, src in [(W4, bank1[0][:, 0:P]), (W34, bank1[0][:, P:2 * P]), (W5, bank1[0][:, 2 * P:3 * P]),
                           (U3, bank1[0][:, 3 * P:4 * P])]:
                step(dve.tensor_copy(wf[w], src))
            step(dve.tensor_scalar(wf[U5H], bank1[1][:, 0:P], 0.5, None, ALU.mult))
            dve.wait_ge(s_pe, C + 3)
            step(dve.tensor_copy(wf[QK], bank1[2][:, 0:P]))
            fence()
            for w in range(NW):
                step(dve.tensor_copy(w_hi[:, w, :], wf[w]))
            fence()
            for w in range(NW):
                step(dve.tensor_tensor(w_lo[:, w, :], wf[w], w_hi[:, w, :].bitcast(F32), ALU.subtract))
            dve.wait_ge(s_act, 1)
            for c in range(C):
                step(dve.tensor_tensor(adj_lo[:, c, :], A_f[c][:], adj_hi[:, c, :].bitcast(F32), ALU.subtract))
                step(dve.tensor_tensor(adjT_lo[:, c, :], At_f[:, c, :], adjT_hi[:, c, :].bitcast(F32), ALU.subtract))
            dve.wait_ge(s_const, 2)
            for c in range(C):
                step(dve.tensor_reduce(deg[:, 0, c:c + 1], B_f[c][:], AX_X, ALU.add))
            fence()
            step(dve.tensor_scalar(deg[:, 1, :], deg[:, 0, :], 0.0, None, ALU.is_gt))
            fence()
            step(dve.tensor_scalar(deg[:, 2, :], deg[:, 1, :], -1.0, 1.0, ALU.mult, ALU.add))
            step(dve.scalar_tensor_tensor(deg[:, 3, :], deg[:, 0, :], 0.0, deg[:, 1, :], ALU.max, ALU.mult))
            fence()
            dve.tensor_tensor(deg[:, 0, :], deg[:, 3, :], deg[:, 2, :], ALU.add).then_inc(s_ones, 1)
            dve.wait_ge(s_const, 3)
            step(dve.tensor_tensor(deg[:, 2, :], deg[:, 4, :], deg[:, 1, :], ALU.mult))
            fence()
            step(dve.tensor_scalar(deg[:, 5, :], deg[:, 2, :], -1.0, None, ALU.mult))
            for c in range(C):
                step(dve.tensor_scalar(B_f[c][:], B_f[c][:], deg[:, 2, c:c + 1], None, ALU.mult))
            fence()
            dve.tensor_copy(deg[:, 3, :], deg[:, 5, :]).then_inc(s_dve, 1)
            for c in range(C):
                dve.wait_ge(s_pool, c + 1)
                dve.scalar_tensor_tensor(lapT_lo[:, c, :], bank0[c][:], deg[:, 5, c:c + 1],
                                         lapT_hi[:, c, :].bitcast(F32), ALU.mult, ALU.subtract).then_inc(s_dve, 1)
            for k in range(LANES):
                dve.tensor_copy(recip[k][:, 0:1], deg[:, 5, 0:1]).then_inc(x_nat_free[k], 1)

            def emit(kind, layer, part, k, at):
                def wait(signal):
                    dve.wait_ge(sig[signal][k], at.now(signal))

                def low(signal, dst, src, hi):
                    dve.tensor_tensor(dst, src, hi.bitcast(F32), ALU.subtract).then_inc(sig[signal][k], 1)

                b0, b1 = bank0[k][:], bank1[k][:]
                key = (kind, part)
                if key == ("X0", 1):
                    wait("n_hi")
                    low("n_lo", n_lo[k][:], x_in[k][:], n_hi[k][:])
                    wait("t_hi")
                    low("t_lo", t_lo[k][:], b0, t_hi[k][:])
                elif key == ("A", 1):
                    wait("m_hi")
                    low("m_lo", m_lo[k][:], b1, m_hi[k][:])
                elif key == ("R", 1):
                    wait("r_tanh")
                    dve.scalar_tensor_tensor(r_buf[k][:], r_buf[k][:], 1.0, hT[k][:], ALU.add, ALU.mult)\
                        .then_inc(sig["rh"][k], 1)
                elif key == ("R", 2):
                    wait("q_hi")
                    low("q_lo", q_lo[k][:], r_buf[k][:], q_hi[k][:])
                elif key == ("U", 1):
                    wait("v_tanh")
                    dve.tensor_tensor(v_buf[k][:], v_buf[k][:], hT[k][:], ALU.subtract)\
                        .then_inc(sig["v_minus_h"][k], 1)
                    wait("v_minus_h")
                    dve.scalar_tensor_tensor(v_buf[k][:], z_buf[k][:], 1.0, v_buf[k][:], ALU.add, ALU.mult)\
                        .then_inc(sig["z_scaled"][k], 1)
                elif key == ("U", 2):
                    wait("z_scaled")
                    dve.scalar_tensor_tensor(hT[k][:], v_buf[k][:], 0.5, hT[k][:], ALU.mult, ALU.add)\
                        .then_inc(sig["h_new"][k], 1)
                elif key == ("T", 1):
                    wait("n_hi")
                    low("n_lo", n_lo[k][:], b0, n_hi[k][:])
                elif kind in ("TL", "ZT", "VT") and part == 1:
                    if kind == "TL":
                        dve.wait_ge(x_nat_free[k], at.g * 16 + 1)
                    wait("bank0")
                    if kind == "VT":
                        for c in range(C):
                            mm = dve.scalar_tensor_tensor(x_nat[k][:, c, :], bank0[k][:, c * P:(c + 1) * P],
                                                          recip[k][:, c:c + 1], x_nat[k][:, c, :],
                                                          ALU.mult, ALU.add)
                    else:
                        mm = dve.tensor_tensor(x_nat[k][:], b0.rearrange("p (c d) -> p c d", c=C),
                                               (x_in if kind == "TL" else x_nat)[k][:], ALU.add)
                    mm.then_inc(sig["summed"][k], 1)
                    wait("summed")
                    for c in range(C):
                        mm = dve.bn_stats(stats[k][:, c, :], x_nat[k][:, c, :])
                    mm.then_inc(sig["stats"][k], 1)
                    wait("stats")
                    dve.tensor_copy(recip[k][:, 0:1], stats[k][:, 0, 1:2])
                    for c in range(C):
                        mm = dve.bn_aggr(moments[k][:, c, :], stats[k][:, c, :])
                    mm.then_inc(sig["moments"][k], 1)
                elif kind in ("TL", "ZT", "VT") and part == 2:
                    wait("rstd")
                    for c in range(C):
                        mm = dve.tensor_scalar(x_nat[k][:, c, :], x_nat[k][:, c, :], moments[k][:, c, 0:1],
                                               rstd[k][:, 1, c:c + 1], ALU.subtract, ALU.mult)
                    mm.then_inc(sig["normed"][k], 1)
                elif kind in ("TL", "ZT", "VT") and part == 3 and layer < 3:
                    wait("n_hi")
                    low("n_lo", n_lo[k][:], x_nat[k][:], n_hi[k][:])
                elif key == ("XA", 1):
                    wait("t_hi")
                    low("t_lo", t_lo[k][:], b0, t_hi[k][:])
                    wait("m_hi")
                    low("m_lo", m_lo[k][:], b1, m_hi[k][:])
                elif key == ("X2", 1):
                    wait("t_hi")
                    low("t_lo", t_lo[k][:], b0, t_hi[k][:])
                elif key == ("YT", 1):
                    wait("n_hi")
                    low("n_lo", n_lo[k][:], b0, n_hi[k][:])
                elif key == ("G", 1):
                    wait("q_hi")
                    low("q_lo", q_lo[k][:], b1, q_hi[k][:])
                elif key == ("S", 1):
                    wait("s_exp")
                    dve.tensor_tensor(r_buf[k][:], r_buf[k][:], At_f[:, layer, :], ALU.mult)\
                        .then_inc(sig["masked"][k], 1)
                elif key == ("S", 2):
                    wait("m_hi")
                    low("m_lo", m_lo[k][:], r_buf[k][:], m_hi[k][:])
                elif key == ("O", 1):
                    wait("m_hi")
                    low("m_lo", m_lo[k][:], b1, m_hi[k][:])
                    wait("bank0")
                    dve.reciprocal(recip[k][:], bank0[k][:, 0:2 * C].rearrange("p (c t) -> p c t", t=2)[:, :, 0])\
                        .then_inc(sig["recip"][k], 1)

            schedule(dve, GROUPS, (0, 1, 2, 3), emit)

        @block.gpsimd
        def _(pool):
            pool.wait_ge(s_ones, 1)
            pool.affine_select(out=ident[:], in_=ones[:], compare_op=ALU.is_equal, fill=0.0, base=0,
                               pattern=[[-1, P]], channel_multiplier=1).then_inc(s_const, 1)
            pool.wait_ge(adj_loaded, 16 * C)
            for c in range(C):
                mm = pool.affine_select(out=B_f[c][:], in_=A_f[c][:], compare_op=ALU.not_equal, fill=0.0,
                                        base=c * P, pattern=[[-1, N]], channel_multiplier=1)
            mm.then_inc(s_const, 1)
            pool.wait_ge(s_dve, 1)
            pool.wait_ge(s_ones, 2)
            pool.tensor_tensor(deg[:, 4, :], deg[:, 0, :], neg_half[:], ALU.pow).then_inc(s_const, 1)

            def emit(kind, layer, part, k, at):
                def wait(signal):
                    pool.wait_ge(sig[signal][k], at.now(signal))

                key = (kind, part)
                if key == ("T", 0):
                    wait("t_hi")
                    pool.tensor_tensor(t_lo[k][:], hT[k][:], t_hi[k][:].bitcast(F32), ALU.subtract)\
                        .then_inc(sig["t_lo"][k], 1)
                elif kind in ("TL", "ZT", "VT") and part == 1:
                    wait("moments")
                    pool.tensor_tensor(rstd[k][:, 0, :], moments[k][:, :, 1], eps[:], ALU.add)\
                        .then_inc(sig["var_eps"][k], 1)
                    wait("var_eps")
                    pool.tensor_tensor(rstd[k][:, 1, :], rstd[k][:, 0, :], neg_half[:], ALU.pow)\
                        .then_inc(sig["rstd"][k], 1)
                elif key == ("S", 1):
                    wait("masked")
                    if layer == 0:
                        pool.tensor_tensor(v_buf[k][:], r_buf[k][:], zeros[:], ALU.add)\
                            .then_inc(sig["e_sum"][k], 1)
                    else:
                        pool.wait_ge(sig["e_sum"][k], at.before("e_sum"))
                        pool.tensor_tensor(v_buf[k][:], v_buf[k][:], r_buf[k][:], ALU.add)\
                            .then_inc(sig["e_sum"][k], 1)

            schedule(pool, GROUPS, (0, 1), emit)


_INS = ['x', 'adj', 'L0_gnn_w3_w', 'L0_gnn_w3_b', 'L0_gnn_u3_w', 'L0_gnn_u3_b', 'L0_gnn_w4_w', 'L0_gnn_w4_b',
        'L0_gnn_w5_w', 'L0_gnn_w5_b', 'L0_gnn_u5_w', 'L0_gnn_u5_b', 'L1_gnn_Theta1', 'L1_gnn_bias',
        'L2_gnn_q', 'L2_gnn_k', 'L2_gnn_v', 'L3_gnn_Ws', 'L3_gnn_bias']


def kernel(**inputs):
    import numpy as _np
    import concourse.bacc as _bacc
    from concourse import mybir as _mybir
    from concourse.bass_utils import run_bass_kernel_spmd as _run

    nc = _bacc.Bacc("TRN2", target_bir_lowering=False, num_devices=1)
    arrays, args = {}, []
    for name in _INS:
        a = _np.ascontiguousarray(inputs[name])
        arrays[f"in_{name}"] = a
        args.append(nc.dram_tensor(f"in_{name}", a.shape, _mybir.dt.from_np(a.dtype), kind="ExternalInput").ap())
    shape = _np.asarray(inputs['x']).shape
    args.append(nc.dram_tensor("out_0", shape, _mybir.dt.float32, kind="ExternalOutput").ap())
    resnorm_gnn(nc, *args)
    r = _run(nc, [arrays], core_ids=[0])
    return r.results[0]["out_0"]
```

```python
from contextlib import ExitStack

import concourse.bass as bass
from concourse import mybir

F32 = mybir.dt.float32
F32R = mybir.dt.float32r
ALU = mybir.AluOpType
ACT = mybir.ActivationFunctionType
AX_X = mybir.AxisListType.X

P = 128
LANES = 4
STEPS = 5
EPS = 1e-5

STAGES = [("X0", 0)]
for step in range(STEPS):
    STAGES += [("A", 0), ("R", 0), ("U", 0), ("T", 0) if step < STEPS - 1 else ("TL", 0)]
STAGES += [("XA", 1), ("Y", 1), ("YT", 1), ("Z", 1), ("ZT", 1)]
STAGES += [("X2", 2), ("G", 2), ("S", 0), ("S", 1), ("S", 2), ("S", 3), ("O", 2), ("V", 2), ("VT", 2)]
STAGES += [("XA", 3), ("Y", 3), ("YT", 3), ("Z", 3), ("ZT3", 3)]
J = len(STAGES)
W = 3 * 0.216
NORM = [
    ("norm summed", "dve", 0.60, "summed", "bank0"),
    ("norm stats", "dve", 0.81, "stats", "summed"),
    ("norm moments", "dve", 0.45, "moments", "stats"),
    ("norm var_eps", "pool", 0.15, "var_eps", "moments"),
    ("norm neg_mean", "pool", 0.15, "neg_mean", "moments"),
    ("norm rstd", "pool", 1.00, "rstd", "var_eps"),
    ("norm shift", "pool", 0.15, "shift", "neg_mean rstd"),
    ("norm normed", "act", 1.44, "normed", "shift"),
]
NORM_SPLIT = [
    ("norm n_hi", "act", 0.484, "n_hi", "normed"),
    ("norm n_lo", "pool", 1.23, "n_lo", "n_hi"),
]
OPS = {
    "X0": [("X0 turn", "pe", 0.43, "bank0", "summed"),
           ("X0 n_hi", "act", 0.484, "n_hi", ""),
           ("X0 t_hi", "act", 0.446, "t_hi", "bank0"),
           ("X0 hT", "act", 0.446, "hT_copied", "bank0"),
           ("X0 n_lo", "dve", 0.60, "n_lo", "n_hi"),
           ("X0 t_lo", "dve", 0.60, "t_lo", "t_hi hT_copied")],
    "A": [("A hi", "pe", 8 * 0.216, None, "n_hi"),
          ("A lo", "pe", 4 * 0.216, "bank1", "n_lo"),
          ("A m_hi", "act", 0.446, "m_hi", "bank1"),
          ("A m_lo", "dve", 0.60, "m_lo", "m_hi")],
    "R": [("R u3", "pe", W, None, "t_hi t_lo"),
          ("R w4", "pe", W, "bank0", "m_hi m_lo"),
          ("R w5", "pe", W, None, "m_lo"),
          ("R r_tanh", "act", 0.446, "r_tanh", "bank0"),
          ("R rh", "dve", 0.60, "rh", "r_tanh"),
          ("R q_hi", "act", 0.484, "q_hi", "rh"),
          ("R q_lo", "dve", 0.60, "q_lo", "q_hi")],
    "U": [("U w34", "pe", W, "bank0", "r_tanh"),
          ("U z_tanh", "act", 0.446, "z_tanh", "bank0"),
          ("U u5", "pe", W, "bank1", "q_lo"),
          ("U h_kept", "dve", 0.60, "h_kept", "z_tanh q_lo"),
          ("U v_tanh", "act", 0.446, "v_tanh", "bank1"),
          ("U v_taken", "dve", 0.60, "v_taken", "v_tanh h_kept"),
          ("U h_new", "dve", 0.60, "h_new", "v_taken")],
    "T": [("T turn", "pe", 0.43, "bank0", "h_new"),
          ("T n_hi", "act", 0.446, "n_hi", "bank0"),
          ("T n_lo", "dve", 0.60, "n_lo", "n_hi"),
          ("T t_hi", "act", 0.484, "t_hi", "h_new"),
          ("T t_lo", "pool", 1.23, "t_lo", "t_hi")],
    "TL": [("T turn", "pe", 0.43, "bank0", "h_new")] + NORM + NORM_SPLIT,
    "XA": [("X turn", "pe", 0.43, "bank0", "normed"),
           ("X t_hi", "act", 0.446, "t_hi", "bank0"),
           ("X t_lo", "dve", 0.60, "t_lo", "t_hi"),
           ("XA hi", "pe", 8 * 0.216, None, "n_hi"),
           ("XA lo", "pe", 4 * 0.216, "bank1", "n_lo"),
           ("XA m_hi", "act", 0.446, "m_hi", "bank1"),
           ("XA m_lo", "dve", 0.60, "m_lo", "m_hi")],
    "Y": [("Y t", "pe", W, None, "t_lo"),
          ("Y m", "pe", W, "bank0", "m_lo"),
          ("Y hT", "act", 0.446, "hT_copied", "bank0")],
    "YT": [("Y turn", "pe", 0.43, "bank0", "hT_copied"),
           ("YT x", "pe", W, None, "t_lo"),
           ("YT n_hi", "act", 0.446, "n_hi", "bank0"),
           ("YT n_lo", "dve", 0.60, "n_lo", "n_hi")],
    "Z": [("Z hi", "pe", 8 * 0.216, None, "n_hi"),
          ("Z lo", "pe", 4 * 0.216, "bank1", "n_lo"),
          ("Z hT", "act", 0.446, "hT_copied", "bank1")],
    "ZT": [("Z turn", "pe", 0.43, "bank0", "hT_copied")] + NORM + NORM_SPLIT,
    "ZT3": [("Z turn", "pe", 0.43, "bank0", "hT_copied")] + NORM + [("ZT store", "act", 0.06, None, "normed")],
    "X2": [("X turn", "pe", 0.43, "bank0", "normed"),
           ("X t_hi", "act", 0.446, "t_hi", "bank0"),
           ("X t_lo", "dve", 0.60, "t_lo", "t_hi")],
    "G": [("G qk", "pe", W, "bank1", "t_lo"),
          ("G q_hi", "act", 0.446, "q_hi", "bank1"),
          ("G q_lo", "dve", 0.60, "q_lo", "q_hi")],
    "S": [("S scores", "pe", W, "bank0", "q_lo"),
          ("S r_tanh", "act", 0.446, "r_tanh", "bank0 e_sum"),
          ("S s_exp", "act", 0.484, "s_exp", "r_tanh"),
          ("S masked", "dve", 0.60, "masked", "s_exp"),
          ("S m_hi", "act", 0.484, "m_hi", "masked"),
          ("S m_lo", "dve", 0.60, "m_lo", "m_hi"),
          ("S e_sum", "pool", 1.23, "e_sum", "masked"),
          ("S sum hi", "pe", 2 * 0.216, None, "m_hi n_lo"),
          ("S sum lo", "pe", 0.216, "bank1", "m_lo")],
    "O": [("O sums", "pe", 0.86, "bank0", "e_sum"),
          ("O m_hi", "act", 0.446, "m_hi", "bank1"),
          ("O m_lo", "dve", 0.60, "m_lo", "m_hi"),
          ("O recip", "dve", 0.10, "recip", "bank0")],
    "V": [("V v", "pe", W, "bank1", "m_lo"),
          ("V hT", "act", 0.446, "hT_copied", "bank1")],
    "VT": [("V turn", "pe", 0.43, "bank0", "hT_copied recip")] + NORM + NORM_SPLIT,
}
GIVEN = {op[3]: {kind for kind in OPS for o in OPS[kind] if o[3] == op[3]}
         for ops in OPS.values() for op in ops if op[3]}
NORMS = 4


def given(signal, j):
    return sum(1 for kind, _ in STAGES[:max(j + 1, 0)] if kind in GIVEN[signal])


OFFSET = (0.0, 4.0, 8.0, 15.0)
HOP = 0.29


def timetable(batches=6):
    ops = [(op, j) for j, (kind, _) in enumerate(STAGES) for op in OPS[kind]]
    n = len(ops)
    after = [[] for _ in ops]
    waits = [0] * n
    last, pe = {}, None
    for i, ((name, engine, us, gives, needs), j) in enumerate(ops):
        before = {last[x]: HOP for x in needs.split() if x in last}
        if engine == "pe":
            if pe is not None:
                before.setdefault(pe, 0.0)
            pe = i
        for d, hop in before.items():
            after[d].append((i, hop))
        waits[i] = len(before)
        if gives:
            last[gives] = i
    way = [0.0] * n
    for i in reversed(range(n)):
        way[i] = ops[i][0][2] + max([way[d] + hop for d, hop in after[i]], default=0.0)

    ready = {e: {} for e in ("pe", "act", "dve", "pool")}
    free = dict.fromkeys(ready, 0.0)
    todo, at, left, begun = {}, {}, {}, {}

    def begin(lane, batch, t):
        left[lane] = n
        for i in range(n):
            todo[lane, i] = waits[i]
            at[lane, i] = t
            if not waits[i]:
                ready[ops[i][0][1]][lane, batch, i] = t

    for lane in range(LANES):
        begin(lane, 0, OFFSET[lane])
    for _ in range(LANES * batches * n):
        t, _, e, key = min((round(max(free[e], t), 6), round(OFFSET[key[0]] + (key[1] + 1) * 240.0 - way[key[2]], 6),
                            e, key) for e in ready for key, t in ready[e].items())
        del ready[e][key]
        lane, batch, i = key
        begun[key] = t
        free[e] = t + ops[i][0][2]
        for d, hop in after[i]:
            at[lane, d] = max(at[lane, d], free[e] + hop)
            todo[lane, d] -= 1
            if not todo[lane, d]:
                ready[ops[d][0][1]][lane, batch, d] = at[lane, d]
        left[lane] -= 1
        if not left[lane] and batch + 1 < batches:
            begin(lane, batch + 1, free[e])

    b = batches - 2
    start = min(begun[lane, b, i] for lane in range(LANES) for i in range(n))
    period = min(begun[lane, b + 1, i] for lane in range(LANES) for i in range(n)) - start
    order = {e: [] for e in ready}
    for lane in range(LANES):
        for i, (op, j) in enumerate(ops):
            t = begun[lane, b, i] - start
            order[op[1]].append((t % period, i, lane, op[0], j, int(t >= period)))
    return {e: [(name, j, lane, before) for _, _, lane, name, j, before in sorted(order[e])] for e in order}


FIRST, MIDDLE, LAST = range(3)


class At:

    def __init__(self, j, period, begun_before):
        self.j, self.period, self.begun_before = j, period, begun_before
        self.first = isinstance(period, int) and period == begun_before

    def upto(self, signal, j):
        return self.batches(given(signal, J - 1), given(signal, j))

    def now(self, signal):
        return self.upto(signal, self.j)

    def before(self, signal):
        return self.upto(signal, self.j - 1)

    def batches(self, each, more):
        assert (self.period if isinstance(self.period, int) else 1) * each + more - self.begun_before * each >= 1
        return self.period * each + (more - self.begun_before * each)

    def row(self, k):
        return self.period * LANES + (k - self.begun_before * LANES)


def run_period(order, period, which, emit):
    for op, j, lane, begun_before in order:
        if which != (FIRST if begun_before else LAST):
            emit(op, *STAGES[j], lane, At(j, period, begun_before))


def schedule(engine, groups, order, emit):
    run_period(order, 0, FIRST, emit)
    with engine.Fori(1, groups) as period:
        run_period(order, period, MIDDLE, emit)
    run_period(order, groups, LAST, emit)


def resnorm_gnn(nc, x, adj, w3_w, w3_b, u3_w, u3_b, w4_w, w4_b, w5_w, w5_b, u5_w, u5_b,
                theta, bias1, q_w, k_w, v_w, ws, bias3, out):
    B, N, D = x.shape
    assert D == P and N % P == 0 and B % LANES == 0
    C = N // P
    GROUPS = B // LANES
    order = timetable()
    SCORE = 1.0 / (8.0 * float(D) ** 0.5)

    with ExitStack() as ctx:
        def sb(name, shape, dt=F32):
            return ctx.enter_context(nc.sbuf_tensor(name, shape, dt))

        def sem(name):
            return ctx.enter_context(nc.semaphore(name))

        def lanes(name, shape, dt=F32):
            return [sb(f"{name}{k}", shape, dt) for k in range(LANES)]

        At_f = sb("At_f", [P, C, N])
        adj_hi, adj_lo = sb("adj_hi", [P, C, N], F32R), sb("adj_lo", [P, C, N], F32R)
        adjT_hi, adjT_lo = sb("adjT_hi", [P, C, N], F32R), sb("adjT_lo", [P, C, N], F32R)
        lapT_hi, lapT_lo = sb("lapT_hi", [P, C, N], F32R), sb("lapT_lo", [P, C, N], F32R)
        ONES_W, W4, W34, W5, U3, U5H, T0, T1, T2, QK, VV, L0, L1, L2 = range(-1, 13)
        NW = 13
        w_hi, w_lo = sb("w_hi", [P, NW, P], F32R), sb("w_lo", [P, NW, P], F32R)
        ident = sb("ident", [P, P])
        ones = sb("ones", [P, P])
        cols = sb("cols", [P, 16])
        bias = sb("bias", [P, 4])
        BR, BZ, BV = range(3)
        neg_half = sb("neg_half", [P, C])
        eps = sb("eps", [P, C])
        zeros = sb("zeros", [P, N])
        deg = sb("deg", [P, 6, C])

        x_in = lanes("x_in", [P, C, P])
        x_nat = lanes("x_nat", [P, C, P])
        n_hi, n_lo = lanes("n_hi", [P, C, P], F32R), lanes("n_lo", [P, C, P], F32R)
        hT = lanes("hT", [P, N])
        t_hi, t_lo = lanes("t_hi", [P, N], F32R), lanes("t_lo", [P, N], F32R)
        m_hi, m_lo = lanes("m_hi", [P, N], F32R), lanes("m_lo", [P, N], F32R)
        q_hi, q_lo = lanes("q_hi", [P, N], F32R), lanes("q_lo", [P, N], F32R)
        r_buf, z_buf, v_buf = lanes("r_buf", [P, N]), lanes("z_buf", [P, N]), lanes("v_buf", [P, N])
        stats = lanes("stats", [P, C, 6])
        moments = lanes("moments", [P, C, 2])
        rstd = lanes("rstd", [P, 4, C])
        recip = lanes("recip", [P, C])

        bank0 = [ctx.enter_context(nc.psum_tensor(f"bank0_{k}", [P, N], F32)) for k in range(LANES)]
        bank1 = [ctx.enter_context(nc.psum_tensor(f"bank1_{k}", [P, N], F32)) for k in range(LANES)]

        sig = {s: [sem(f"{s}_{k}") for k in range(LANES)] for s in GIVEN}
        loaded = [sem(f"loaded_{k}") for k in range(LANES)]
        x_nat_free = [sem(f"x_nat_free_{k}") for k in range(LANES)]
        adj_loaded = sem("adj_loaded")
        w_loaded = sem("w_loaded")
        s_const = sem("s_const")
        s_ones = sem("s_ones")
        s_pe = sem("s_pe")
        s_dve = sem("s_dve")
        s_act = sem("s_act")
        s_pool = sem("s_pool")

        A_f = [r_buf[c] for c in range(C)]
        B_f = [z_buf[c] for c in range(C)]
        wraw = [x_nat[k] for k in range(LANES)]
        wsum = v_buf

        adj_rows = adj.rearrange("(c p) n -> p c n", p=P)
        x_rows = x.rearrange("b (c p) d -> b p c d", p=P)
        out_rows = out.rearrange("b (c p) d -> b p c d", p=P)

        block = ctx.enter_context(nc.Block())

        def raw(i):
            return wraw[i // C][:, i % C, :]
        R_W3A, R_W3B, R_W4A, R_W4B, R_W5A, R_W5B, R_U3, R_U5, R_Q, R_K = range(10)
        R_TH = 10
        ws_raw = hT[0]
        v_raw = hT[1]

        @block.sync
        def _(sp):
            for c in range(C):
                sp.dma_start(A_f[c][:], adj_rows[:, c, :]).then_inc(adj_loaded, 16)
            for dst, src in [(R_W3A, w3_w[:, 0:P]), (R_W3B, w3_w[:, P:2 * P]), (R_W4A, w4_w[:, 0:P]),
                             (R_W4B, w4_w[:, P:2 * P]), (R_W5A, w5_w[:, 0:P]), (R_W5B, w5_w[:, P:2 * P]),
                             (R_U3, u3_w), (R_U5, u5_w), (R_Q, q_w), (R_K, k_w)]:
                sp.dma_start(raw(dst), src).then_inc(w_loaded, 16)
            for t in range(5):
                sp.dma_start(raw(R_TH + t), theta[t * P:(t + 1) * P, :]).then_inc(w_loaded, 16)
            sp.dma_start(ws_raw[:, 0:3 * P].rearrange("p (k o) -> p k o", k=3),
                         ws.rearrange("k f o -> f k o")).then_inc(w_loaded, 16)
            sp.dma_start(v_raw[:, 0:P], v_w).then_inc(w_loaded, 16)
            for n, b in enumerate([w3_b, w4_b, w5_b, u3_b, u5_b, bias1, bias3]):
                sp.dma_start(cols[:, n:n + 1], b.rearrange("(p a) -> p a", a=1)).then_inc(w_loaded, 16)
            for k in range(LANES):
                sp.dma_start(x_in[k][:], x_rows[k]).then_inc(loaded[k], 16)
            with sp.Fori(0, GROUPS - 1) as g:
                for k in range(LANES):
                    sp.wait_ge(sig["summed"][k], g * NORMS + 1)
                    src = x_rows[bass.ds(g * LANES + (k + LANES), 1)].rearrange("a p c d -> (a p) c d")
                    sp.dma_start(x_in[k][:], src).then_inc(loaded[k], 16)
            for k in range(LANES):
                sp.wait_ge(x_nat_free[k], 16 * GROUPS + 1)

        W_ALL = 16 * (10 + 5 + 2 + 7)

        @block.tensor
        def _(pe):
            def three(dst, st_hi, st_lo, mv_hi, mv_lo, start, stop, shared=False):
                pe.matmul(dst, st_hi, mv_hi, start=start, stop=False, skip_group_check=shared)
                pe.matmul(dst, st_hi, mv_lo, start=False, stop=False, skip_group_check=shared)
                return pe.matmul(dst, st_lo, mv_hi, start=False, stop=stop, skip_group_check=shared)

            pe.wait_ge(s_const, 1)
            pe.wait_ge(adj_loaded, 16 * C)
            for c in range(C):
                for r in range(C):
                    mm = pe.transpose(bank0[c][:, r * P:(r + 1) * P], A_f[r][:, c * P:(c + 1) * P], ident[:])
                mm.then_inc(s_pe, 1)
            pe.wait_ge(w_loaded, W_ALL)
            pe.wait_ge(s_dve, 2)
            for n, src in enumerate([wsum[0][:, 0:P], wsum[0][:, P:2 * P], wsum[0][:, 2 * P:3 * P], raw(R_U3)]):
                mm = pe.transpose(bank1[0][:, n * P:(n + 1) * P], src, ident[:])
            mm.then_inc(s_pe, 1)
            for n, src in enumerate([raw(R_U5), raw(R_Q), raw(R_K)]):
                mm = pe.transpose(bank1[1][:, n * P:(n + 1) * P], src, ident[:])
            mm.then_inc(s_pe, 1)
            pe.wait_ge(s_dve, 3)
            pe.matmul(bank1[2][:, 0:P], wsum[1][:, 0:P], wsum[1][:, P:2 * P], start=True, stop=True).then_inc(s_pe, 1)
            pe.wait_ge(s_dve, 4)
            pe.wait_ge(s_act, 1)
            for c in range(C):
                for r in range(C):
                    mm = pe.transpose(bank0[c][:, r * P:(r + 1) * P], B_f[r][:, c * P:(c + 1) * P], ident[:])
                mm.then_inc(s_pe, 1)
            pe.wait_ge(s_dve, 4 + C)
            pe.wait_ge(s_act, 2)

            def emit(op, kind, layer, k, at):
                def need(signal):
                    pe.wait_ge(sig[signal][k], at.before(signal))

                b0, b1 = bank0[k][:], bank1[k][:]

                def transposes(src):
                    for c in range(C):
                        mm = pe.transpose(bank0[k][:, c * P:(c + 1) * P], src(c), ident[:])
                    mm.then_inc(sig["bank0"][k], 1)

                def rows_hi(dst, mv_hi, mv_lo, start):
                    need("n_hi")
                    for c in range(C):
                        pe.matmul(dst, n_hi[k][:, c, :], mv_hi[:, c, :], start=start and c == 0, stop=False)
                        pe.matmul(dst, n_hi[k][:, c, :], mv_lo[:, c, :], start=False, stop=False)

                def rows_lo(dst, mv_hi):
                    need("n_lo")
                    for c in range(C):
                        mm = pe.matmul(dst, n_lo[k][:, c, :], mv_hi[:, c, :], start=False, stop=(c == C - 1))
                    mm.then_inc(sig["bank1"][k], 1)

                def weight(dst, w, mv_hi, mv_lo, start, stop, shared=False):
                    return three(dst, w_hi[:, w, :], w_lo[:, w, :], mv_hi[k][:], mv_lo[k][:], start, stop, shared)

                mix_hi, mix_lo = (adj_hi, adj_lo) if layer == 1 else (lapT_hi, lapT_lo)
                if op == "X0 turn":
                    if not at.first:
                        need("summed")
                    pe.wait_ge(loaded[k], at.batches(16, 16))
                    transposes(lambda c: x_in[k][:, c, :])
                if op == "A hi":
                    if at.j == 1:
                        need("t_lo")
                    rows_hi(b1, adjT_hi, adjT_lo, True)
                if op == "A lo":
                    rows_lo(b1, adjT_hi)
                if op == "R u3":
                    need("t_hi")
                    need("t_lo")
                    weight(b0, U3, t_hi, t_lo, True, False)
                if op == "R w4":
                    need("m_hi")
                    need("m_lo")
                    weight(b0, W4, m_hi, m_lo, False, True).then_inc(sig["bank0"][k], 1)
                if op == "R w5":
                    weight(b1, W5, m_hi, m_lo, True, False)
                if op == "U w34":
                    need("r_tanh")
                    weight(b0, W34, m_hi, m_lo, False, True, shared=True).then_inc(sig["bank0"][k], 1)
                if op == "U u5":
                    need("q_hi")
                    need("q_lo")
                    weight(b1, U5H, q_hi, q_lo, False, True).then_inc(sig["bank1"][k], 1)
                if op == "T turn":
                    need("h_new")
                    transposes(lambda c: hT[k][:, c * P:(c + 1) * P])
                if op == "X turn":
                    need("normed")
                    transposes(lambda c: x_nat[k][:, c, :])
                if op == "XA hi":
                    rows_hi(b1, mix_hi, mix_lo, True)
                if op == "XA lo":
                    rows_lo(b1, mix_hi)
                if op == "Y t":
                    need("t_hi")
                    need("t_lo")
                    weight(b0, T1 if layer == 1 else L1, t_hi, t_lo, True, False)
                if op == "Y m":
                    need("m_hi")
                    need("m_lo")
                    weight(b0, T2 if layer == 1 else L2, m_hi, m_lo, False, True).then_inc(sig["bank0"][k], 1)
                if op in ("Y turn", "Z turn", "V turn"):
                    need("hT_copied")
                    if op == "V turn":
                        need("recip")
                    transposes(lambda c: hT[k][:, c * P:(c + 1) * P])
                if op == "YT x":
                    weight(b1, T0 if layer == 1 else L0, t_hi, t_lo, True, False)
                if op == "Z hi":
                    rows_hi(b1, mix_hi, mix_lo, False)
                if op == "Z lo":
                    rows_lo(b1, mix_hi)
                if op == "G qk":
                    need("t_hi")
                    need("t_lo")
                    weight(b1, QK, t_hi, t_lo, True, True).then_inc(sig["bank1"][k], 1)
                if op == "S scores":
                    if layer == 0:
                        need("q_hi")
                        need("q_lo")
                    s = slice(layer * P, (layer + 1) * P)
                    three(b0, t_hi[k][:, s], t_lo[k][:, s], q_hi[k][:], q_lo[k][:], True, True)\
                        .then_inc(sig["bank0"][k], 1)
                if op == "S sum hi":
                    pe.wait_ge(sig["m_hi"][k], at.now("m_hi"))
                    if layer == 0:
                        need("n_hi")
                        need("n_lo")
                    pe.matmul(b1, n_hi[k][:, layer, :], m_hi[k][:], start=(layer == 0), stop=False)
                    pe.matmul(b1, n_lo[k][:, layer, :], m_hi[k][:], start=False, stop=False)
                if op == "S sum lo":
                    pe.wait_ge(sig["m_lo"][k], at.now("m_lo"))
                    pe.matmul(b1, n_hi[k][:, layer, :], m_lo[k][:], start=False, stop=(layer == C - 1))\
                        .then_inc(sig["bank1"][k], 1)
                if op == "O sums":
                    need("e_sum")
                    for r in range(C):
                        mm = pe.matmul(bank0[k][:, 2 * r:2 * r + 2], v_buf[k][:, r * P:(r + 1) * P],
                                       ones[:, 0:2], start=True, stop=True)
                    mm.then_inc(sig["bank0"][k], 1)
                if op == "V v":
                    need("m_hi")
                    need("m_lo")
                    weight(b1, VV, m_hi, m_lo, True, True).then_inc(sig["bank1"][k], 1)

            schedule(pe, GROUPS, order["pe"], emit)

        @block.scalar
        def _(act):
            act.wait_ge(adj_loaded, 16 * C)
            for c in range(C):
                act.activation(adj_hi[:, c, :], A_f[c][:], ACT.Copy)
            for c in range(C):
                act.wait_ge(s_pe, c + 1)
                act.activation(At_f[:, c, :], bank0[c][:], ACT.Copy)
                mm = act.activation(adjT_hi[:, c, :], bank0[c][:], ACT.Copy)
            mm.then_inc(s_act, 1)
            act.wait_ge(s_dve, 4)
            for c in range(C):
                act.wait_ge(s_pe, 7 + c + 1)
                mm = act.activation(lapT_hi[:, c, :], bank0[c][:], ACT.Copy, scale=deg[:, 5, c:c + 1])
                mm.then_inc(s_pool, 1)
            act.wait_ge(s_dve, 4)
            act.activation(cols[:, 8:9], cols[:, 0:1], ACT.Exp).then_inc(s_act, 1)

            def emit(op, kind, layer, k, at):
                def wait(signal):
                    act.wait_ge(sig[signal][k], at.now(signal))

                def copy(signal, dst, src):
                    act.activation(dst, src, ACT.Copy).then_inc(sig[signal][k], 1)

                b0, b1 = bank0[k][:], bank1[k][:]
                if op == "X0 n_hi":
                    act.wait_ge(loaded[k], at.batches(16, 16))
                    act.activation(n_hi[k][:], x_in[k][:], ACT.Copy, scale=2.0).then_inc(sig["n_hi"][k], 1)
                if op == "X0 t_hi":
                    wait("bank0")
                    act.activation(t_hi[k][:], b0, ACT.Copy, scale=2.0).then_inc(sig["t_hi"][k], 1)
                if op == "X0 hT":
                    wait("bank0")
                    act.activation(hT[k][:], b0, ACT.Copy, scale=2.0).then_inc(sig["hT_copied"][k], 1)
                if op == "A m_hi":
                    wait("bank1")
                    copy("m_hi", m_hi[k][:], b1)
                if op == "R r_tanh":
                    wait("bank0")
                    act.activation(r_buf[k][:], b0, ACT.Tanh, bias=bias[:, BR:BR + 1], scale=0.5)\
                        .then_inc(sig["r_tanh"][k], 1)
                if op == "R q_hi":
                    wait("rh")
                    copy("q_hi", q_hi[k][:], r_buf[k][:])
                if op == "U z_tanh":
                    wait("bank0")
                    act.activation(z_buf[k][:], b0, ACT.Tanh, bias=bias[:, BZ:BZ + 1], scale=0.5)\
                        .then_inc(sig["z_tanh"][k], 1)
                if op == "U v_tanh":
                    wait("bank1")
                    act.activation(v_buf[k][:], b1, ACT.Tanh, bias=bias[:, BV:BV + 1]).then_inc(sig["v_tanh"][k], 1)
                if op == "T n_hi":
                    wait("bank0")
                    copy("n_hi", n_hi[k][:], b0)
                if op == "T t_hi":
                    wait("h_new")
                    copy("t_hi", t_hi[k][:], hT[k][:])
                if op == "norm normed":
                    wait("shift")
                    for c in range(C):
                        mm = act.activation(x_nat[k][:, c, :], x_nat[k][:, c, :], ACT.Identity,
                                            bias=rstd[k][:, 3, c:c + 1], scale=rstd[k][:, 2, c:c + 1])
                    mm.then_inc(sig["normed"][k], 1)
                if op == "norm n_hi":
                    wait("normed")
                    copy("n_hi", n_hi[k][:], x_nat[k][:])
                if op == "ZT store":
                    wait("normed")
                    dst = out_rows[bass.ds(at.row(k), 1)].rearrange("a p c d -> (a p) c d")
                    act.dma_start(dst, x_nat[k][:]).then_inc(x_nat_free[k], 16)
                if op == "X t_hi":
                    wait("bank0")
                    copy("t_hi", t_hi[k][:], b0)
                if op == "XA m_hi":
                    wait("bank1")
                    copy("m_hi", m_hi[k][:], b1)
                if op == "Y hT":
                    wait("bank0")
                    copy("hT_copied", hT[k][:], b0)
                if op == "YT n_hi":
                    wait("bank0")
                    copy("n_hi", n_hi[k][:], b0)
                if op == "Z hT":
                    wait("bank1")
                    act.activation(hT[k][:], b1, ACT.Relu if layer == 1 else ACT.Identity,
                                   bias=cols[:, 5:6] if layer == 1 else cols[:, 6:7])\
                        .then_inc(sig["hT_copied"][k], 1)
                if op == "G q_hi":
                    wait("bank1")
                    copy("q_hi", q_hi[k][:], b1)
                if op == "S m_hi":
                    wait("masked")
                    copy("m_hi", m_hi[k][:], r_buf[k][:])
                if op == "S r_tanh":
                    if layer > 0:
                        act.wait_ge(sig["e_sum"][k], at.before("e_sum"))
                    wait("bank0")
                    act.activation(r_buf[k][:], b0, ACT.Tanh, scale=SCORE).then_inc(sig["r_tanh"][k], 1)
                if op == "S s_exp":
                    wait("r_tanh")
                    act.activation(r_buf[k][:], r_buf[k][:], ACT.Exp, scale=8.0).then_inc(sig["s_exp"][k], 1)
                if op == "O m_hi":
                    wait("bank1")
                    copy("m_hi", m_hi[k][:], b1)
                if op == "V hT":
                    wait("bank1")
                    copy("hT_copied", hT[k][:], b1)

            schedule(act, GROUPS, order["act"], emit)

        @block.vector
        def _(dve):
            own = sem("own_dve")
            n_own = [0]

            def step(ins):
                n_own[0] += 1
                ins.then_inc(own, 1)

            def fence():
                dve.wait_ge(own, n_own[0])

            dve.memset(ones[:], 1.0).then_inc(s_ones, 1)
            dve.memset(eps[:], EPS)
            dve.memset(zeros[:], 0.0)
            dve.memset(neg_half[:], -0.5).then_inc(s_dve, 1)
            dve.wait_ge(w_loaded, W_ALL)
            step(dve.tensor_tensor(wsum[0][:, 0:P], raw(R_W4A), raw(R_W4B), ALU.add))
            step(dve.tensor_tensor(wsum[0][:, 3 * P:4 * P], raw(R_W3A), raw(R_W3B), ALU.add))
            fence()
            step(dve.tensor_tensor(wsum[0][:, P:2 * P], wsum[0][:, 3 * P:4 * P], wsum[0][:, 0:P], ALU.subtract))
            fence()
            dve.tensor_tensor(wsum[0][:, 2 * P:3 * P], raw(R_W5A), raw(R_W5B), ALU.add).then_inc(s_dve, 1)
            wf = [hT[2][:, 0:P], hT[2][:, P:2 * P], hT[2][:, 2 * P:3 * P], hT[2][:, 3 * P:4 * P],
                  hT[3][:, 0:P], hT[3][:, P:2 * P], hT[3][:, 2 * P:3 * P], hT[3][:, 3 * P:4 * P],
                  wsum[2][:, 0:P], wsum[2][:, P:2 * P], wsum[2][:, 2 * P:3 * P], wsum[2][:, 3 * P:4 * P],
                  wsum[3][:, 0:P]]
            tmp = wsum[3][:, P:2 * P]
            step(dve.tensor_tensor(tmp, raw(R_TH + 2), raw(R_TH + 4), ALU.add))
            fence()
            step(dve.tensor_tensor(wf[T0], raw(R_TH), tmp, ALU.subtract))
            step(dve.tensor_scalar(wf[T2], tmp, 2.0, None, ALU.mult))
            step(dve.tensor_tensor(wf[T1], raw(R_TH + 1), raw(R_TH + 3), ALU.add))
            step(dve.tensor_tensor(wf[L0], ws_raw[:, 0:P], ws_raw[:, 2 * P:3 * P], ALU.subtract))
            step(dve.tensor_copy(wf[L1], ws_raw[:, P:2 * P]))
            step(dve.tensor_scalar(wf[L2], ws_raw[:, 2 * P:3 * P], 2.0, None, ALU.mult))
            step(dve.tensor_copy(wf[VV], v_raw[:, 0:P]))
            step(dve.tensor_tensor(cols[:, 9:10], cols[:, 1:2], cols[:, 3:4], ALU.add))
            step(dve.tensor_tensor(cols[:, 10:11], cols[:, 0:1], cols[:, 3:4], ALU.add))
            step(dve.tensor_tensor(bias[:, BV:BV + 1], cols[:, 2:3], cols[:, 4:5], ALU.add))
            fence()
            step(dve.tensor_scalar(bias[:, BR:BR + 1], cols[:, 9:10], 0.5, None, ALU.mult))
            step(dve.tensor_scalar(bias[:, BZ:BZ + 1], cols[:, 10:11], 0.5, None, ALU.mult))
            dve.wait_ge(s_pe, C + 2)
            dve.tensor_copy(wsum[1][:, 0:2 * P], bank1[1][:, P:3 * P]).then_inc(s_dve, 1)
            for w, src in [(W4, bank1[0][:, 0:P]), (W34, bank1[0][:, P:2 * P]), (W5, bank1[0][:, 2 * P:3 * P]),
                           (U3, bank1[0][:, 3 * P:4 * P])]:
                step(dve.tensor_scalar(wf[w], src, 0.5, None, ALU.mult))
            step(dve.tensor_scalar(wf[U5H], bank1[1][:, 0:P], 0.25, None, ALU.mult))
            dve.wait_ge(s_pe, C + 3)
            step(dve.tensor_copy(wf[QK], bank1[2][:, 0:P]))
            fence()
            for w in range(NW):
                step(dve.tensor_copy(w_hi[:, w, :], wf[w]))
            fence()
            for w in range(NW):
                step(dve.tensor_tensor(w_lo[:, w, :], wf[w], w_hi[:, w, :].bitcast(F32), ALU.subtract))
            dve.wait_ge(s_act, 1)
            for c in range(C):
                step(dve.tensor_tensor(adj_lo[:, c, :], A_f[c][:], adj_hi[:, c, :].bitcast(F32), ALU.subtract))
                step(dve.tensor_tensor(adjT_lo[:, c, :], At_f[:, c, :], adjT_hi[:, c, :].bitcast(F32), ALU.subtract))
            dve.wait_ge(s_const, 2)
            for c in range(C):
                step(dve.tensor_reduce(deg[:, 0, c:c + 1], B_f[c][:], AX_X, ALU.add))
            fence()
            step(dve.tensor_scalar(deg[:, 1, :], deg[:, 0, :], 0.0, None, ALU.is_gt))
            fence()
            step(dve.tensor_scalar(deg[:, 2, :], deg[:, 1, :], -1.0, 1.0, ALU.mult, ALU.add))
            step(dve.scalar_tensor_tensor(deg[:, 3, :], deg[:, 0, :], 0.0, deg[:, 1, :], ALU.max, ALU.mult))
            fence()
            dve.tensor_tensor(deg[:, 0, :], deg[:, 3, :], deg[:, 2, :], ALU.add).then_inc(s_ones, 1)
            dve.wait_ge(s_const, 3)
            step(dve.tensor_tensor(deg[:, 2, :], deg[:, 4, :], deg[:, 1, :], ALU.mult))
            fence()
            step(dve.tensor_scalar(deg[:, 5, :], deg[:, 2, :], -1.0, None, ALU.mult))
            for c in range(C):
                step(dve.tensor_scalar(B_f[c][:], B_f[c][:], deg[:, 2, c:c + 1], None, ALU.mult))
            fence()
            dve.tensor_copy(deg[:, 3, :], deg[:, 5, :]).then_inc(s_dve, 1)
            for c in range(C):
                dve.wait_ge(s_pool, c + 1)
                dve.scalar_tensor_tensor(lapT_lo[:, c, :], bank0[c][:], deg[:, 5, c:c + 1],
                                         lapT_hi[:, c, :].bitcast(F32), ALU.mult, ALU.subtract).then_inc(s_dve, 1)
            for k in range(LANES):
                dve.tensor_copy(recip[k][:, 0:1], deg[:, 5, 0:1]).then_inc(x_nat_free[k], 1)

            def emit(op, kind, layer, k, at):
                def wait(signal):
                    dve.wait_ge(sig[signal][k], at.now(signal))

                def low(signal, dst, src, hi):
                    dve.tensor_tensor(dst, src, hi.bitcast(F32), ALU.subtract).then_inc(sig[signal][k], 1)

                b0, b1 = bank0[k][:], bank1[k][:]
                if op == "X0 t_lo":
                    wait("t_hi")
                    wait("hT_copied")
                    low("t_lo", t_lo[k][:], hT[k][:], t_hi[k][:])
                if op == "X0 n_lo":
                    wait("n_hi")
                    dve.scalar_tensor_tensor(n_lo[k][:], x_in[k][:], 2.0, n_hi[k][:].bitcast(F32),
                                             ALU.mult, ALU.subtract).then_inc(sig["n_lo"][k], 1)
                if op == "A m_lo":
                    wait("m_hi")
                    low("m_lo", m_lo[k][:], b1, m_hi[k][:])
                if op == "R q_lo":
                    wait("q_hi")
                    low("q_lo", q_lo[k][:], r_buf[k][:], q_hi[k][:])
                if op == "R rh":
                    wait("r_tanh")
                    dve.scalar_tensor_tensor(r_buf[k][:], r_buf[k][:], 1.0, hT[k][:], ALU.add, ALU.mult)\
                        .then_inc(sig["rh"][k], 1)
                if op == "U h_new":
                    wait("v_taken")
                    dve.scalar_tensor_tensor(hT[k][:], r_buf[k][:], -0.5, v_buf[k][:], ALU.mult, ALU.add)\
                        .then_inc(sig["h_new"][k], 1)
                if op == "U h_kept":
                    dve.wait_ge(sig["q_lo"][k], at.before("q_lo"))
                    wait("z_tanh")
                    dve.scalar_tensor_tensor(r_buf[k][:], z_buf[k][:], 1.0, hT[k][:], ALU.subtract, ALU.mult)\
                        .then_inc(sig["h_kept"][k], 1)
                if op == "U v_taken":
                    wait("v_tanh")
                    dve.scalar_tensor_tensor(v_buf[k][:], z_buf[k][:], 1.0, v_buf[k][:], ALU.add, ALU.mult)\
                        .then_inc(sig["v_taken"][k], 1)
                if op == "T n_lo":
                    wait("n_hi")
                    low("n_lo", n_lo[k][:], b0, n_hi[k][:])
                if op == "norm summed":
                    if kind == "TL":
                        dve.wait_ge(x_nat_free[k], at.batches(16, 1))
                    wait("bank0")
                    if kind == "VT":
                        for c in range(C):
                            mm = dve.scalar_tensor_tensor(x_nat[k][:, c, :], bank0[k][:, c * P:(c + 1) * P],
                                                          recip[k][:, c:c + 1], x_nat[k][:, c, :],
                                                          ALU.mult, ALU.add)
                    elif kind == "TL":
                        mm = dve.scalar_tensor_tensor(x_nat[k][:].rearrange("p c d -> p (c d)"), b0, 0.5,
                                                      x_in[k][:].rearrange("p c d -> p (c d)"), ALU.mult, ALU.add)
                    else:
                        mm = dve.tensor_tensor(x_nat[k][:], b0.rearrange("p (c d) -> p c d", c=C), x_nat[k][:], ALU.add)
                    mm.then_inc(sig["summed"][k], 1)
                if op == "norm stats":
                    wait("summed")
                    for c in range(C):
                        mm = dve.bn_stats(stats[k][:, c, :], x_nat[k][:, c, :])
                    mm.then_inc(sig["stats"][k], 1)
                if op == "norm moments":
                    wait("stats")
                    dve.tensor_copy(recip[k][:, 0:1], stats[k][:, 0, 1:2])
                    for c in range(C):
                        mm = dve.bn_aggr(moments[k][:, c, :], stats[k][:, c, :])
                    mm.then_inc(sig["moments"][k], 1)
                if op == "X t_lo":
                    wait("t_hi")
                    low("t_lo", t_lo[k][:], b0, t_hi[k][:])
                if op == "XA m_lo":
                    wait("m_hi")
                    low("m_lo", m_lo[k][:], b1, m_hi[k][:])
                if op == "YT n_lo":
                    wait("n_hi")
                    low("n_lo", n_lo[k][:], b0, n_hi[k][:])
                if op == "G q_lo":
                    wait("q_hi")
                    low("q_lo", q_lo[k][:], b1, q_hi[k][:])
                if op == "S masked":
                    wait("s_exp")
                    dve.tensor_tensor(r_buf[k][:], r_buf[k][:], At_f[:, layer, :], ALU.mult)\
                        .then_inc(sig["masked"][k], 1)
                if op == "S m_lo":
                    wait("m_hi")
                    low("m_lo", m_lo[k][:], r_buf[k][:], m_hi[k][:])
                if op == "O m_lo":
                    wait("m_hi")
                    low("m_lo", m_lo[k][:], b1, m_hi[k][:])
                if op == "O recip":
                    wait("bank0")
                    dve.reciprocal(recip[k][:], bank0[k][:, 0:2 * C].rearrange("p (c t) -> p c t", t=2)[:, :, 0])\
                        .then_inc(sig["recip"][k], 1)

            schedule(dve, GROUPS, order["dve"], emit)

        @block.gpsimd
        def _(pool):
            pool.wait_ge(s_ones, 1)
            pool.affine_select(out=ident[:], in_=ones[:], compare_op=ALU.is_equal, fill=0.0, base=0,
                               pattern=[[-1, P]], channel_multiplier=1).then_inc(s_const, 1)
            pool.wait_ge(adj_loaded, 16 * C)
            for c in range(C):
                mm = pool.affine_select(out=B_f[c][:], in_=A_f[c][:], compare_op=ALU.not_equal, fill=0.0,
                                        base=c * P, pattern=[[-1, N]], channel_multiplier=1)
            mm.then_inc(s_const, 1)
            pool.wait_ge(s_dve, 1)
            pool.wait_ge(s_ones, 2)
            pool.tensor_tensor(deg[:, 4, :], deg[:, 0, :], neg_half[:], ALU.pow).then_inc(s_const, 1)

            def emit(op, kind, layer, k, at):
                def wait(signal):
                    pool.wait_ge(sig[signal][k], at.now(signal))

                def low(signal, dst, src, hi):
                    pool.tensor_tensor(dst, src, hi.bitcast(F32), ALU.subtract).then_inc(sig[signal][k], 1)

                if op == "T t_lo":
                    wait("t_hi")
                    low("t_lo", t_lo[k][:], hT[k][:], t_hi[k][:])
                if op == "norm var_eps":
                    wait("moments")
                    pool.tensor_tensor(rstd[k][:, 0, :], moments[k][:, :, 1], eps[:], ALU.add)\
                        .then_inc(sig["var_eps"][k], 1)
                if op == "norm neg_mean":
                    wait("moments")
                    pool.tensor_tensor(rstd[k][:, 1, :], zeros[:, 0:C], moments[k][:, :, 0], ALU.subtract)\
                        .then_inc(sig["neg_mean"][k], 1)
                if op == "norm rstd":
                    wait("var_eps")
                    pool.tensor_tensor(rstd[k][:, 2, :], rstd[k][:, 0, :], neg_half[:], ALU.pow)\
                        .then_inc(sig["rstd"][k], 1)
                if op == "norm shift":
                    wait("neg_mean")
                    wait("rstd")
                    pool.tensor_tensor(rstd[k][:, 3, :], rstd[k][:, 1, :], rstd[k][:, 2, :], ALU.mult)\
                        .then_inc(sig["shift"][k], 1)
                if op == "norm n_lo":
                    wait("n_hi")
                    low("n_lo", n_lo[k][:], x_nat[k][:], n_hi[k][:])
                if op == "S e_sum":
                    wait("masked")
                    if layer == 0:
                        pool.tensor_tensor(v_buf[k][:], r_buf[k][:], zeros[:], ALU.add)\
                            .then_inc(sig["e_sum"][k], 1)
                    else:
                        pool.wait_ge(sig["e_sum"][k], at.before("e_sum"))
                        pool.tensor_tensor(v_buf[k][:], v_buf[k][:], r_buf[k][:], ALU.add)\
                            .then_inc(sig["e_sum"][k], 1)

            schedule(pool, GROUPS, order["pool"], emit)


_INS = ['x', 'adj', 'L0_gnn_w3_w', 'L0_gnn_w3_b', 'L0_gnn_u3_w', 'L0_gnn_u3_b', 'L0_gnn_w4_w', 'L0_gnn_w4_b',
        'L0_gnn_w5_w', 'L0_gnn_w5_b', 'L0_gnn_u5_w', 'L0_gnn_u5_b', 'L1_gnn_Theta1', 'L1_gnn_bias',
        'L2_gnn_q', 'L2_gnn_k', 'L2_gnn_v', 'L3_gnn_Ws', 'L3_gnn_bias']


def kernel(**inputs):
    import numpy as _np
    import concourse.bacc as _bacc
    from concourse import mybir as _mybir
    from concourse.bass_utils import run_bass_kernel_spmd as _run

    nc = _bacc.Bacc("TRN2", target_bir_lowering=False, num_devices=1)
    arrays, args = {}, []
    for name in _INS:
        a = _np.ascontiguousarray(inputs[name])
        arrays[f"in_{name}"] = a
        args.append(nc.dram_tensor(f"in_{name}", a.shape, _mybir.dt.from_np(a.dtype), kind="ExternalInput").ap())
    shape = _np.asarray(inputs['x']).shape
    args.append(nc.dram_tensor("out_0", shape, _mybir.dt.float32, kind="ExternalOutput").ap())
    resnorm_gnn(nc, *args)
    r = _run(nc, [arrays], core_ids=[0])
    return r.results[0]["out_0"]
```

```python
from contextlib import ExitStack

import concourse.bass as bass
from concourse import mybir

F32 = mybir.dt.float32
F32R = mybir.dt.float32r
ALU = mybir.AluOpType
ACT = mybir.ActivationFunctionType
AX_X = mybir.AxisListType.X

P = 128
LANES = 4
STEPS = 5
EPS = 1e-5

STAGES = [("X0", 0)]
for step in range(STEPS):
    STAGES += [("A", 0), ("R", 0), ("U", 0), ("T", 0) if step < STEPS - 1 else ("TL", 0)]
STAGES += [("XA", 1), ("Y", 1), ("YT", 1), ("Z", 1), ("ZT", 1)]
STAGES += [("X2", 2), ("G", 2), ("S", 0), ("S", 1), ("S", 2), ("SL", 3), ("O", 2), ("V", 2), ("VT", 2)]
STAGES += [("XA", 3), ("Y", 3), ("YT", 3), ("Z", 3), ("ZT3", 3)]
J = len(STAGES)
W = 3 * 0.216
NORM = [
    ("norm summed", "dve", 0.60, "summed", "bank0"),
    ("norm stats", "dve", 0.81, "stats", "summed"),
    ("norm moments", "dve", 0.37, "moments", "stats"),
    ("norm var_eps", "pool", 0.15, "var_eps", "moments"),
    ("norm rstd", "pool", 0.96, "rstd", "var_eps"),
    ("norm normed", "dve", 1.03, "normed", "rstd"),
]
NORM_SPLIT = [
    ("norm n_hi", "act", 0.52, "n_hi", "normed"),
    ("norm n_lo", "pool", 1.23, "n_lo", "n_hi"),
]
BLOCK = [
    ("S r_tanh", "act", 0.48, "r_tanh", "bank0 e_sum@2"),
    ("S s_exp", "act", 0.52, "s_exp", "r_tanh"),
    ("S masked", "dve", 0.60, "masked", "s_exp"),
    ("S m_hi", "act", 0.52, "m_hi", "masked bank1"),
    ("S m_lo", "dve", 0.60, "m_lo", "m_hi"),
    ("S e_sum", "pool", 1.23, "e_sum", "masked"),
    ("S sum hi", "pe", 2 * 0.216, None, "m_hi n_lo"),
    ("S sum lo", "pe", 0.216, "bank1", "m_lo"),
]
OPS = {
    "X0": [("X0 turn", "pe", 0.43, "bank0", "summed"),
           ("X0 n_hi", "act", 0.52, "n_hi", ""),
           ("X0 t_hi", "act", 0.48, "t_hi", "bank0"),
           ("X0 hT", "act", 0.48, "hT_copied", "bank0"),
           ("X0 n_lo", "dve", 0.60, "n_lo", "n_hi"),
           ("X0 t_lo", "dve", 0.60, "t_lo", "t_hi hT_copied")],
    "A": [("A hi", "pe", 8 * 0.216, None, "n_hi"),
          ("A lo", "pe", 4 * 0.216, "bank1", "n_lo"),
          ("A m_hi", "act", 0.48, "m_hi", "bank1"),
          ("A m_lo", "dve", 0.60, "m_lo", "m_hi")],
    "R": [("R u3", "pe", W, None, "t_hi t_lo"),
          ("R w4", "pe", W, "bank0", "m_hi m_lo"),
          ("R w5", "pe", W, None, "m_lo"),
          ("R r_tanh", "act", 0.57, "r_tanh", "bank0"),
          ("R rh", "dve", 0.60, "rh", "r_tanh"),
          ("R q_hi", "act", 0.52, "q_hi", "rh"),
          ("R q_lo", "dve", 0.60, "q_lo", "q_hi")],
    "U": [("U w34", "pe", W, "bank0", "r_tanh"),
          ("U z_tanh", "act", 0.57, "z_tanh", "bank0"),
          ("U u5", "pe", W, "bank1", "q_lo"),
          ("U h_kept", "dve", 0.60, "h_kept", "z_tanh q_lo"),
          ("U v_tanh", "act", 0.57, "v_tanh", "bank1"),
          ("U v_taken", "dve", 0.60, "v_taken", "v_tanh h_kept"),
          ("U h_new", "dve", 0.60, "h_new", "v_taken")],
    "T": [("T turn", "pe", 0.43, "bank0", "h_new"),
          ("T n_hi", "act", 0.48, "n_hi", "bank0"),
          ("T n_lo", "dve", 0.60, "n_lo", "n_hi"),
          ("T t_hi", "act", 0.52, "t_hi", "h_new"),
          ("T t_lo", "pool", 1.23, "t_lo", "t_hi")],
    "TL": [("T turn", "pe", 0.43, "bank0", "h_new")] + NORM + NORM_SPLIT,
    "XA": [("X turn", "pe", 0.43, "bank0", "normed"),
           ("X t_hi", "act", 0.48, "t_hi", "bank0"),
           ("X t_lo", "dve", 0.60, "t_lo", "t_hi"),
           ("XA hi", "pe", 8 * 0.216, None, "n_hi"),
           ("XA lo", "pe", 4 * 0.216, "bank1", "n_lo"),
           ("XA m_hi", "act", 0.48, "m_hi", "bank1"),
           ("XA m_lo", "dve", 0.60, "m_lo", "m_hi")],
    "Y": [("Y t", "pe", W, None, "t_lo"),
          ("Y m", "pe", W, "bank0", "m_lo"),
          ("Y hT", "act", 0.48, "hT_copied", "bank0")],
    "YT": [("Y turn", "pe", 0.43, "bank0", "hT_copied"),
           ("YT x", "pe", W, None, "t_lo"),
           ("YT n_hi", "act", 0.48, "n_hi", "bank0"),
           ("YT n_lo", "dve", 0.60, "n_lo", "n_hi")],
    "Z": [("Z hi", "pe", 8 * 0.216, None, "n_hi"),
          ("Z lo", "pe", 4 * 0.216, "bank1", "n_lo"),
          ("Z hT", "act", 0.57, "hT_copied", "bank1")],
    "ZT": [("Z turn", "pe", 0.43, "bank0", "hT_copied")] + NORM + NORM_SPLIT,
    "ZT3": [("Z turn", "pe", 0.43, "bank0", "hT_copied")] + NORM + [("ZT store", "act", 0.06, None, "normed")],
    "X2": [("X turn", "pe", 0.43, "bank0", "normed"),
           ("X t_hi", "act", 0.48, "t_hi", "bank0"),
           ("X t_lo", "dve", 0.60, "t_lo", "t_hi")],
    "G": [("G qk", "pe", W, "bank1", "t_lo"),
          ("G q_hi", "act", 0.48, "q_hi", "bank1"),
          ("G q_lo", "dve", 0.60, "q_lo", "q_hi"),
          ("G scores", "pe", W, "bank0", "q_lo")],
    "S": BLOCK[:3] + [("S scores", "pe", W, "bank0", "r_tanh")] + BLOCK[3:],
    "SL": BLOCK,
    "O": [("O sums", "pe", 0.75, "bank0", "e_sum"),
          ("O m_hi", "act", 0.48, "m_hi", "bank1"),
          ("O m_lo", "dve", 0.60, "m_lo", "m_hi"),
          ("O recip", "dve", 0.10, "recip", "bank0")],
    "V": [("V v", "pe", W, "bank1", "m_lo"),
          ("V hT", "act", 0.48, "hT_copied", "bank1")],
    "VT": [("V turn", "pe", 0.43, "bank0", "hT_copied recip")] + NORM + NORM_SPLIT,
}
GIVEN = {op[3]: {kind for kind in OPS for o in OPS[kind] if o[3] == op[3]}
         for ops in OPS.values() for op in ops if op[3]}
NORMS = 4


def given(signal, j):
    return sum(1 for kind, _ in STAGES[:max(j + 1, 0)] if kind in GIVEN[signal])


BLOCKS = range(4)
LATE = {}
for c in BLOCKS:
    LATE["adj hi", c] = ("act", 0.52, [])
    LATE["adj lo", c] = ("pool", 1.23, [("adj hi", c)])
    LATE["diagonal", c] = ("pool", 0.60, [("adj lo", c)])
    LATE["degree", c] = ("dve", 0.60, [("diagonal", c)])
LATE["weights a", 0] = ("pool", 0.90, [])
LATE["weights b", 0] = ("pool", 1.00, [("weights a", 0)])
LATE["weights hi", 0] = ("act", 0.90, [("weights b", 0)])
LATE["weights lo", 0] = ("dve", 1.10, [("weights hi", 0)])
LATE["positive", 0] = ("dve", 0.10, [("degree", c) for c in BLOCKS])
LATE["safe a", 0] = ("dve", 0.15, [("positive", 0)])
LATE["safe b", 0] = ("dve", 0.10, [("safe a", 0)])
LATE["pow", 0] = ("pool", 0.96, [("safe b", 0)])
LATE["dinv", 0] = ("dve", 0.10, [("pow", 0)])
LATE["dinv row", 0] = ("dma", 5.00, [("dinv", 0)])
LATE["negative", 0] = ("dve", 0.10, [("dinv", 0)])
for c in BLOCKS:
    LATE["adjT", c] = ("pool", 1.23, [])
    LATE["lap rows", c] = ("pool", 1.23, [("adjT", c), ("dinv row", 0)])
    LATE["lap diagonal", c] = ("pool", 0.60, [("lap rows", c)])
    LATE["lap hi", c] = ("act", 0.52, [("lap diagonal", c), ("negative", 0)])
    LATE["lap lo", c] = ("dve", 0.60, [("lap hi", c)])
LATE_FOR = {("XA hi", 1): [("adj lo", c) for c in BLOCKS], ("Y t", 1): [("weights lo", 0)],
            ("XA hi", 3): [("lap lo", c) for c in BLOCKS]}
LATE_FOR.update({("S masked", c): [("adjT", c)] for c in BLOCKS})

LATE_START = 25.0
DEADLINE = (0.0, 19.1, 12.5, 29.2)
START = (0.0, 0, 3.3, 9.9)
TURN = 287.8
HOP = {"pe": 0.386, "act": 0.127, "dve": 0.112, "pool": 0.243, "dma": 0.0}
URGENT = {
    "S scores": -1.9, "S m_lo": -0.6, "Z turn": 3.6, "XA hi": -4.1, "A hi": -1.9, "U h_kept": 8.2, "R w5": -0.3,
    "norm normed": 2.3, "Y turn": 4.2, "U u5": 0.9, "S m_hi": 3.1, "G q_lo": 5.4, "A lo": 1.5, "S sum lo": -0.9,
    "O m_hi": -10.5, "R q_hi": -0.4, "V v": 1.0, "X t_hi": 8.7, "Y t": 0.6, "X turn": 2.2, "U v_tanh": -1.0,
    "R q_lo": -0.2, "X0 t_lo": 10.0, "norm stats": -3.6, "G q_hi": -0.7, "S r_tanh": -4.8, "O m_lo": 3.9,
    "R r_tanh": 2.8, "norm rstd": 2.1, "R w4": -0.1, "X0 turn": -1.9, "norm moments": 4.5, "O recip": -0.4,
    "U z_tanh": 3.9, "S s_exp": 2.8, "U v_taken": -2.6, "V hT": -3.3, "norm var_eps": 2.0, "R u3": 1.2,
    "A m_lo": 5.1, "T t_lo": 5.6, "V turn": 3.4, "U w34": 0.4, "norm summed": 1.0, "G scores": 7.5, "T n_lo": -5.9,
    "X0 hT": 0.2, "Y m": 0.2, "S e_sum": 0.2, "Z lo": -3.1, "U h_new": 4.1, "XA m_lo": 13.0, "T n_hi": -1.1,
    "X0 t_hi": 3.9, "X0 n_lo": -3.0, "Z hT": -0.1, "Y hT": 8.9, "X0 n_hi": 1.6, "R rh": -2.1, "norm n_hi": -9.7,
    "XA m_hi": -5.0, "T turn": 1.7, "YT n_lo": -5.2, "YT x": -2.9, "A m_hi": 1.0, "norm n_lo": -0.2, "O sums": -2.4,
    "YT n_hi": 6.5, "T t_hi": 3.3, "S masked": -6.0, "ZT store": -3.3, "Z hi": -0.8, "X t_lo": -3.4,
    "S sum hi": -0.5,
}


def play(nodes, urgency, start):
    after = {key: [] for key in nodes}
    waits, at, begun = {}, {}, {}
    free = dict.fromkeys(HOP, 0.0)
    ready = {e: set() for e in HOP}
    for key, (e, _, before) in nodes.items():
        before = [b for b in before if b in nodes]
        for b in before:
            after[b].append(key)
        waits[key], at[key] = len(before), start.get(key, 0.0)
        if not before:
            ready[e].add(key)

    def choice(e):
        return min(((round(max(free[e], at[key]), 6), round(urgency[key], 6), e, str(key), key) for key in ready[e]),
                   default=None)

    choices = {e: choice(e) for e in HOP}
    while any(choices.values()):
        t, _, e, _, key = min(x for x in choices.values() if x)
        ready[e].remove(key)
        begun[key] = t
        free[e] = t + nodes[key][1]
        changed = {e}
        for n in after[key]:
            d = nodes[n][0]
            at[n] = max(at[n], free[e] + (0.0 if d == e == "pe" else HOP[d]))
            waits[n] -= 1
            if not waits[n]:
                ready[d].add(n)
                changed.add(d)
        for d in changed:
            choices[d] = choice(d)
    return begun


def timetable(batches=5):
    ops = [(op, j) for j, (kind, _) in enumerate(STAGES) for op in OPS[kind]]
    n = len(ops)
    follows = [[] for _ in ops]
    last = {}
    for i, ((name, engine, us, gives, needs), j) in enumerate(ops):
        follows[i] = [last[x] for x in needs.split() if x in last]
        if gives and gives in last:
            last[gives + "@2"] = last[gives]
        if engine == "pe":
            follows[i] += [last["pe"]] if "pe" in last else []
            last["pe"] = i
        if gives:
            last[gives] = i
    way = [0.0] * n
    for i in reversed(range(n)):
        way[i] += ops[i][0][2]
        for b in follows[i]:
            way[b] = max(way[b], way[i] + (0.0 if ops[b][0][1] == ops[i][0][1] == "pe" else HOP[ops[i][0][1]]))
    between = {0: [last["summed"], last["pe"]], 1: [last["hT_copied"]]}
    assert [ops[i][0][0] for i in between] == ["X0 turn", "X0 n_hi"]

    nodes, urgency = {}, {}
    for batch in range(batches):
        for lane in range(LANES):
            for i, ((name, engine, us, _, _), j) in enumerate(ops):
                before = [(lane, batch, b) for b in follows[i]]
                if batch:
                    before += [(lane, batch - 1, b) for b in between.get(i, [])]
                nodes[lane, batch, i] = (engine, us, before)
                urgency[lane, batch, i] = DEADLINE[lane] + (batch + 1) * TURN - way[i] - URGENT.get(name, 0.0)
    start = {(lane, 0, i): START[lane] for lane in range(LANES) for i in between}
    begun = play(nodes, urgency, start)
    b = batches - 2
    origin = min(begun[lane, b, i] for lane in range(LANES) for i in range(n))
    period = min(begun[lane, b + 1, i] for lane in range(LANES) for i in range(n)) - origin
    assert max(begun[lane, b, i] for lane in range(LANES) for i in range(n)) < origin + 2 * period

    def parts(before):
        return {(lane, 0, i) for lane in range(LANES) for i in range(n)
                if (begun[lane, b, i] - origin >= period) == before}

    first = {key: nodes[key] for key in parts(False)}
    assert set(LATE_FOR) <= {(ops[i][0][0], STAGES[ops[i][1]][1]) for _, _, i in parts(False)}
    for key, (engine, us, before) in first.items():
        (name, *_), j = ops[key[2]]
        wanted = LATE_FOR.get((name, STAGES[j][1]), [])
        first[key] = (engine, us, before + wanted)
        for late in wanted:
            urgency[late] = min(urgency.get(late, 1e9), urgency[key] - 1.0)
    for late in reversed(LATE):
        urgency.setdefault(late, 1e9)
        for x in LATE[late][2]:
            urgency[x] = min(urgency.get(x, 1e9), urgency[late] - LATE[late][1] - 1.0)
    first.update(LATE)
    start.update(dict.fromkeys(LATE, LATE_START))
    first = play(first, urgency, start)
    final = play({key: nodes[key] for key in parts(True)}, urgency, {})

    begun_before = parts(True)

    def entries(times, engine):
        order = sorted((t, key) for key, t in times.items()
                       if (LATE[key] if len(key) == 2 else nodes[key])[0] == engine)
        return [key if len(key) == 2 else (ops[key[2]][0][0], ops[key[2]][1], key[0], int(key in begun_before))
                for _, key in order]

    middle = {(lane, 0, i): (begun[lane, b, i] - origin) % period for lane in range(LANES) for i in range(n)}
    return {e: [entries(times, e) for times in (first, middle, final)]
            for e in ("pe", "act", "dve", "pool")}


class At:

    def __init__(self, j, period, begun_before):
        self.j, self.period, self.begun_before = j, period, begun_before
        self.first = isinstance(period, int) and period == begun_before

    def upto(self, signal, j):
        return self.batches(given(signal, J - 1), given(signal, j))

    def now(self, signal):
        return self.upto(signal, self.j)

    def before(self, signal):
        return self.upto(signal, self.j - 1)

    def batches(self, each, more):
        assert (self.period if isinstance(self.period, int) else 1) * each + more - self.begun_before * each >= 1
        return self.period * each + (more - self.begun_before * each)

    def row(self, k):
        return self.period * LANES + (k - self.begun_before * LANES)


def schedule(engine, groups, order, emit, emit_late=None):
    def run(entries, period):
        for entry in entries:
            if len(entry) == 2:
                emit_late(*entry)
            else:
                op, j, lane, begun_before = entry
                emit(op, *STAGES[j], lane, At(j, period, begun_before))

    first, middle, final = order
    run(first, 0)
    with engine.Fori(1, groups) as period:
        run(middle, period)
    run(final, groups)


def resnorm_gnn(nc, x, adj, w3_w, w3_b, u3_w, u3_b, w4_w, w4_b, w5_w, w5_b, u5_w, u5_b,
                theta, bias1, q_w, k_w, v_w, ws, bias3, out):
    B, N, D = x.shape
    assert D == P and N % P == 0 and B % LANES == 0
    C = N // P
    GROUPS = B // LANES
    order = timetable()
    SCORE = 1.0 / (8.0 * float(D) ** 0.5)

    with ExitStack() as ctx:
        def sb(name, shape, dt=F32):
            return ctx.enter_context(nc.sbuf_tensor(name, shape, dt))

        def sem(name):
            return ctx.enter_context(nc.semaphore(name))

        def lanes(name, shape, dt=F32):
            return [sb(f"{name}{k}", shape, dt) for k in range(LANES)]

        At_f = sb("At_f", [P, C, N])
        A_f = sb("A_f", [P, C, N])
        dinv_row = sb("dinv_row", [P, P, C])
        late_raw = sb("late_raw", [P, 9, P])
        late_w = sb("late_w", [P, 7, P])
        adj_hi, adj_lo = sb("adj_hi", [P, C, N], F32R), sb("adj_lo", [P, C, N], F32R)
        adjT_hi, adjT_lo = sb("adjT_hi", [P, C, N], F32R), sb("adjT_lo", [P, C, N], F32R)
        lapT_hi, lapT_lo = sb("lapT_hi", [P, C, N], F32R), sb("lapT_lo", [P, C, N], F32R)
        W4, W34, W5, U3, U5H, QK, T0, T1, T2, VV, L0, L1, L2 = range(13)
        NW = 13
        w_hi, w_lo = sb("w_hi", [P, NW, P], F32R), sb("w_lo", [P, NW, P], F32R)
        ident = sb("ident", [P, P])
        ones = sb("ones", [P, P])
        cols = sb("cols", [P, 16])
        bias = sb("bias", [P, 4])
        BR, BZ, BV = range(3)
        neg_half = sb("neg_half", [P, C])
        eps = sb("eps", [P, C])
        zeros = sb("zeros", [P, N])
        deg = sb("deg", [P, 7, C])

        x_in = lanes("x_in", [P, C, P])
        x_nat = lanes("x_nat", [P, C, P])
        n_hi, n_lo = lanes("n_hi", [P, C, P], F32R), lanes("n_lo", [P, C, P], F32R)
        hT = lanes("hT", [P, N])
        t_hi, t_lo = lanes("t_hi", [P, N], F32R), lanes("t_lo", [P, N], F32R)
        m_hi, m_lo = lanes("m_hi", [P, N], F32R), lanes("m_lo", [P, N], F32R)
        q_hi, q_lo = lanes("q_hi", [P, N], F32R), lanes("q_lo", [P, N], F32R)
        r_buf, z_buf, v_buf = lanes("r_buf", [P, N]), lanes("z_buf", [P, N]), lanes("v_buf", [P, N])
        stats = lanes("stats", [P, C, 6])
        moments = lanes("moments", [P, C, 2])
        rstd = lanes("rstd", [P, 2, C])
        recip = lanes("recip", [P, C])

        bank0 = [ctx.enter_context(nc.psum_tensor(f"bank0_{k}", [P, N], F32)) for k in range(LANES)]
        bank1 = [ctx.enter_context(nc.psum_tensor(f"bank1_{k}", [P, N], F32)) for k in range(LANES)]

        sig = {s: [sem(f"{s}_{k}") for k in range(LANES)] for s in GIVEN}
        loaded = [sem(f"loaded_{k}") for k in range(LANES)]
        x_nat_free = [sem(f"x_nat_free_{k}") for k in range(LANES)]
        adj_loaded = [sem(f"adj_loaded_{c}") for c in range(C)]
        w_loaded = sem("w_loaded")
        bias_loaded, late_loaded = sem("bias_loaded"), sem("late_loaded")
        ident_ready, consts_ready = sem("ident_ready"), sem("consts_ready")
        w_summed, w_turned = sem("w_summed"), sem("w_turned")
        w_hi_ready = sem("w_hi_ready")
        w_lo_ready = sem("w_lo_ready")
        adj_turned = sem("adj_turned")
        adjT_hi_ready, adjT_lo_ready = sem("adjT_hi_ready"), sem("adjT_lo_ready")
        bias_steps = sem("bias_steps")
        adj_hi_ready, adj_lo_ready = sem("adj_hi_ready"), sem("adj_lo_ready")
        adjT_ready = sem("adjT_ready")
        late_w_steps = sem("late_w_steps")
        diag_cleared = sem("diag_cleared")
        dinv_steps, pow_ready = sem("dinv_steps"), sem("pow_ready")
        DEGREES, IS_POSITIVE, SAFE_PARTS, IS_SAFE, HAS_DINV, HAS_NEGATIVE = C, C + 1, C + 3, C + 4, C + 5, C + 6
        dinv_moved = sem("dinv_moved")
        lap_rows_ready, lap_ready = sem("lap_rows_ready"), sem("lap_ready")
        lapT_hi_ready, lapT_lo_ready = sem("lapT_hi_ready"), sem("lapT_lo_ready")

        w4_raw, w3_raw, w5_raw = (z_buf[k][:, 0:2 * P] for k in range(3))
        u3_raw, u5_raw = z_buf[3][:, 0:P], z_buf[3][:, P:2 * P]
        q_raw, k_raw = z_buf[3][:, 2 * P:3 * P], z_buf[3][:, 3 * P:4 * P]
        w_sum = v_buf[0]
        qkT = v_buf[1]
        DEG, POSITIVE, ZERO, SAFE, POW, DINV, NEG_DINV = range(7)
        dinv_dram = nc.dram_tensor("dinv_scratch", (N,), F32, kind="Internal").ap()

        adj_rows = adj.rearrange("(c p) n -> p c n", p=P)
        x_rows = x.rearrange("b (c p) d -> b p c d", p=P)
        out_rows = out.rearrange("b (c p) d -> b p c d", p=P)

        block = ctx.enter_context(nc.Block())

        @block.sync
        def _(sp):
            for c in range(C):
                sp.dma_start(A_f[:, c, :], adj_rows[:, c, :]).then_inc(adj_loaded[c], 16)
            sp.dma_start(x_in[0][:], x_rows[0]).then_inc(loaded[0], 16)
            for dst, src in [(u5_raw, u5_w), (q_raw, q_w), (k_raw, k_w)]:
                sp.dma_start(dst, src).then_inc(w_loaded, 16)
            for n, b in enumerate([w3_b, w4_b, w5_b, u3_b, u5_b, bias1, bias3]):
                sp.dma_start(cols[:, n:n + 1], b.rearrange("(p a) -> p a", a=1)).then_inc(bias_loaded, 16)
            for k in range(1, LANES):
                sp.dma_start(x_in[k][:], x_rows[k]).then_inc(loaded[k], 16)
            sp.dma_start(late_raw[:, 0:5, :], theta.rearrange("(t f) o -> f t o", f=P)).then_inc(late_loaded, 16)
            sp.dma_start(late_raw[:, 5:8, :], ws.rearrange("k f o -> f k o")).then_inc(late_loaded, 16)
            sp.dma_start(late_raw[:, 8, :], v_w).then_inc(late_loaded, 16)
            sp.wait_ge(dinv_steps, HAS_DINV)
            sp.dma_start(dinv_dram.rearrange("(p c) -> p c", c=C), deg[:, DINV, :]).then_inc(dinv_moved, 16)
            sp.wait_ge(dinv_moved, 16)
            sp.dma_start(dinv_row[:].rearrange("q p c -> q (p c)"), dinv_dram.partition_broadcast(P))\
                .then_inc(dinv_moved, 16)
            with sp.Fori(0, GROUPS - 1) as g:
                for k in range(LANES):
                    sp.wait_ge(sig["summed"][k], g * NORMS + 1)
                    src = x_rows[bass.ds(g * LANES + (k + LANES), 1)].rearrange("a p c d -> (a p) c d")
                    sp.dma_start(x_in[k][:], src).then_inc(loaded[k], 16)
            for k in range(LANES):
                sp.wait_ge(x_nat_free[k], 16 * GROUPS)

        @block.tensor
        def _(pe):
            def three(dst, st_hi, st_lo, mv_hi, mv_lo, start, stop, shared=False):
                pe.matmul(dst, st_hi, mv_hi, start=start, stop=False, skip_group_check=shared)
                pe.matmul(dst, st_hi, mv_lo, start=False, stop=False, skip_group_check=shared)
                return pe.matmul(dst, st_lo, mv_hi, start=False, stop=stop, skip_group_check=shared)

            pe.wait_ge(ident_ready, 1)
            for r in range(C):
                pe.wait_ge(adj_loaded[r], 16)
                for c in range(C):
                    mm = pe.transpose(bank0[c][:, r * P:(r + 1) * P], A_f[:, r, c * P:(c + 1) * P], ident[:])
                    if r == C - 1:
                        mm.then_inc(adj_turned, 1)
            pe.wait_ge(w_loaded, 16 * 7)
            for n, src in enumerate([u5_raw, q_raw, k_raw]):
                mm = pe.transpose(bank1[2][:, n * P:(n + 1) * P], src, ident[:])
            mm.then_inc(w_turned, 1)
            pe.wait_ge(w_summed, 4)
            for n, src in enumerate([w_sum[:, 0:P], w_sum[:, P:2 * P], w_sum[:, 2 * P:3 * P], u3_raw]):
                mm = pe.transpose(bank1[3][:, n * P:(n + 1) * P], src, ident[:])
            mm.then_inc(w_turned, 1)
            pe.wait_ge(w_hi_ready, 2)
            pe.matmul(bank1[1][:, 0:P], qkT[:, 0:P], qkT[:, P:2 * P], start=True, stop=True).then_inc(w_turned, 1)

            def emit(op, kind, layer, k, at):
                def need(signal):
                    pe.wait_ge(sig[signal][k], at.before(signal))

                b0, b1 = bank0[k][:], bank1[k][:]

                def transposes(src):
                    for c in range(C):
                        mm = pe.transpose(bank0[k][:, c * P:(c + 1) * P], src(c), ident[:])
                    mm.then_inc(sig["bank0"][k], 1)

                def rows_hi(dst, mv_hi, mv_lo, start):
                    need("n_hi")
                    for c in range(C):
                        pe.matmul(dst, n_hi[k][:, c, :], mv_hi[:, c, :], start=start and c == 0, stop=False)
                        pe.matmul(dst, n_hi[k][:, c, :], mv_lo[:, c, :], start=False, stop=False)

                def rows_lo(dst, mv_hi):
                    need("n_lo")
                    for c in range(C):
                        mm = pe.matmul(dst, n_lo[k][:, c, :], mv_hi[:, c, :], start=False, stop=(c == C - 1))
                    mm.then_inc(sig["bank1"][k], 1)

                def weight(dst, w, mv_hi, mv_lo, start, stop, shared=False):
                    return three(dst, w_hi[:, w, :], w_lo[:, w, :], mv_hi[k][:], mv_lo[k][:], start, stop, shared)

                mix_hi, mix_lo = (adj_hi, adj_lo) if layer == 1 else (lapT_hi, lapT_lo)
                if op == "X0 turn":
                    if at.first:
                        pe.wait_ge(adjT_hi_ready, k + 1)
                        pe.wait_ge(adjT_lo_ready, k + 1)
                    if not at.first:
                        need("summed")
                    pe.wait_ge(loaded[k], at.batches(16, 16))
                    transposes(lambda c: x_in[k][:, c, :])
                if op == "A hi":
                    if at.first and at.j == 1:
                        pe.wait_ge(adjT_hi_ready, C)
                        pe.wait_ge(adjT_lo_ready, C)
                        if k == 1:
                            pe.wait_ge(w_hi_ready, 4)
                            pe.wait_ge(w_lo_ready, 3)
                    rows_hi(b1, adjT_hi, adjT_lo, True)
                if op == "A lo":
                    rows_lo(b1, adjT_hi)
                if op == "R u3":
                    if at.first and at.j == 2 and k == 0:
                        pe.wait_ge(w_hi_ready, 3)
                        pe.wait_ge(w_lo_ready, 2)
                    need("t_hi")
                    need("t_lo")
                    weight(b0, U3, t_hi, t_lo, True, False)
                if op == "R w4":
                    need("m_hi")
                    need("m_lo")
                    weight(b0, W4, m_hi, m_lo, False, True).then_inc(sig["bank0"][k], 1)
                if op == "R w5":
                    weight(b1, W5, m_hi, m_lo, True, False)
                if op == "U w34":
                    need("r_tanh")
                    weight(b0, W34, m_hi, m_lo, False, True, shared=True).then_inc(sig["bank0"][k], 1)
                if op == "U u5":
                    need("q_hi")
                    need("q_lo")
                    weight(b1, U5H, q_hi, q_lo, False, True).then_inc(sig["bank1"][k], 1)
                if op == "T turn":
                    need("h_new")
                    transposes(lambda c: hT[k][:, c * P:(c + 1) * P])
                if op == "X turn":
                    need("normed")
                    transposes(lambda c: x_nat[k][:, c, :])
                if op == "XA hi":
                    if at.first and layer == 1:
                        pe.wait_ge(adj_hi_ready, C)
                        pe.wait_ge(adj_lo_ready, C)
                    if at.first and layer == 3:
                        pe.wait_ge(lapT_hi_ready, C)
                        pe.wait_ge(lapT_lo_ready, C)
                    rows_hi(b1, mix_hi, mix_lo, True)
                if op == "XA lo":
                    rows_lo(b1, mix_hi)
                if op == "Y t":
                    if at.first:
                        pe.wait_ge(w_hi_ready, 5)
                        pe.wait_ge(w_lo_ready, 4)
                    need("t_hi")
                    need("t_lo")
                    weight(b0, T1 if layer == 1 else L1, t_hi, t_lo, True, False)
                if op == "Y m":
                    need("m_hi")
                    need("m_lo")
                    weight(b0, T2 if layer == 1 else L2, m_hi, m_lo, False, True).then_inc(sig["bank0"][k], 1)
                if op in ("Y turn", "Z turn", "V turn"):
                    need("hT_copied")
                    if op == "V turn":
                        need("recip")
                    transposes(lambda c: hT[k][:, c * P:(c + 1) * P])
                if op == "YT x":
                    weight(b1, T0 if layer == 1 else L0, t_hi, t_lo, True, False)
                if op == "Z hi":
                    rows_hi(b1, mix_hi, mix_lo, False)
                if op == "Z lo":
                    rows_lo(b1, mix_hi)
                if op == "G qk":
                    need("t_hi")
                    need("t_lo")
                    weight(b1, QK, t_hi, t_lo, True, True).then_inc(sig["bank1"][k], 1)
                if op in ("G scores", "S scores"):
                    if op == "G scores":
                        pe.wait_ge(sig["q_hi"][k], at.now("q_hi"))
                        pe.wait_ge(sig["q_lo"][k], at.now("q_lo"))
                        s = slice(0, P)
                    else:
                        pe.wait_ge(sig["r_tanh"][k], at.now("r_tanh"))
                        s = slice((layer + 1) * P, (layer + 2) * P)
                    three(b0, t_hi[k][:, s], t_lo[k][:, s], q_hi[k][:], q_lo[k][:], True, True)\
                        .then_inc(sig["bank0"][k], 1)
                if op == "S sum hi":
                    pe.wait_ge(sig["m_hi"][k], at.now("m_hi"))
                    if layer == 0:
                        need("n_hi")
                        need("n_lo")
                    pe.matmul(b1, n_hi[k][:, layer, :], m_hi[k][:], start=(layer == 0), stop=False)
                    pe.matmul(b1, n_lo[k][:, layer, :], m_hi[k][:], start=False, stop=False)
                if op == "S sum lo":
                    pe.wait_ge(sig["m_lo"][k], at.now("m_lo"))
                    pe.matmul(b1, n_hi[k][:, layer, :], m_lo[k][:], start=False, stop=(layer == C - 1))\
                        .then_inc(sig["bank1"][k], 1)
                if op == "O sums":
                    need("e_sum")
                    for r in range(C):
                        mm = pe.matmul(bank0[k][:, 2 * r:2 * r + 2], v_buf[k][:, r * P:(r + 1) * P],
                                       ones[:, 0:2], start=True, stop=True)
                    mm.then_inc(sig["bank0"][k], 1)
                if op == "V v":
                    need("m_hi")
                    need("m_lo")
                    weight(b1, VV, m_hi, m_lo, True, True).then_inc(sig["bank1"][k], 1)

            schedule(pe, GROUPS, order["pe"], emit)

        @block.scalar
        def _(act):
            for dst, src in [(w4_raw, w4_w), (w3_raw, w3_w), (w5_raw, w5_w), (u3_raw, u3_w)]:
                act.dma_start(dst, src).then_inc(w_loaded, 16)
            for c in range(C):
                act.wait_ge(adj_turned, c + 1)
                act.activation(adjT_hi[:, c, :], bank0[c][:], ACT.Copy).then_inc(adjT_hi_ready, 1)
            act.wait_ge(w_turned, 1)
            act.activation(w_hi[:, U5H, :], bank1[2][:, 0:P], ACT.Copy, scale=0.25).then_inc(w_hi_ready, 1)
            act.activation(qkT[:, 0:2 * P], bank1[2][:, P:3 * P], ACT.Copy).then_inc(w_hi_ready, 1)
            act.wait_ge(w_turned, 2)
            act.activation(w_hi[:, W4:U3 + 1, :], bank1[3][:].rearrange("p (w o) -> p w o", o=P), ACT.Copy, scale=0.5)\
                .then_inc(w_hi_ready, 1)
            act.wait_ge(w_turned, 3)
            act.activation(w_hi[:, QK, :], bank1[1][:, 0:P], ACT.Copy).then_inc(w_hi_ready, 1)

            def late(what, c):
                if what == "adj hi":
                    act.wait_ge(adj_loaded[c], 16)
                    act.activation(adj_hi[:, c, :], A_f[:, c, :], ACT.Copy).then_inc(adj_hi_ready, 1)
                if what == "weights hi":
                    act.wait_ge(late_w_steps, 8)
                    act.activation(w_hi[:, T0:L2 + 1, :], late_w[:], ACT.Copy).then_inc(w_hi_ready, 1)
                if what == "lap hi":
                    act.wait_ge(lap_ready, c + 1)
                    act.wait_ge(dinv_steps, HAS_NEGATIVE)
                    act.activation(lapT_hi[:, c, :], A_f[:, c, :], ACT.Copy, scale=deg[:, NEG_DINV, c:c + 1])\
                        .then_inc(lapT_hi_ready, 1)

            def emit(op, kind, layer, k, at):
                def wait(signal):
                    act.wait_ge(sig[signal][k], at.now(signal))

                def copy(signal, dst, src):
                    act.activation(dst, src, ACT.Copy).then_inc(sig[signal][k], 1)

                b0, b1 = bank0[k][:], bank1[k][:]
                e_buf = (r_buf, z_buf)[layer % 2][k][:]
                if op == "X0 n_hi":
                    act.wait_ge(loaded[k], at.batches(16, 16))
                    act.activation(n_hi[k][:], x_in[k][:], ACT.Copy, scale=2.0).then_inc(sig["n_hi"][k], 1)
                if op == "X0 t_hi":
                    wait("bank0")
                    act.activation(t_hi[k][:], b0, ACT.Copy, scale=2.0).then_inc(sig["t_hi"][k], 1)
                if op == "X0 hT":
                    wait("bank0")
                    act.activation(hT[k][:], b0, ACT.Copy, scale=2.0).then_inc(sig["hT_copied"][k], 1)
                if op == "A m_hi":
                    wait("bank1")
                    copy("m_hi", m_hi[k][:], b1)
                if op == "R r_tanh":
                    if at.first and at.j == 2:
                        act.wait_ge(bias_steps, 5)
                    wait("bank0")
                    act.activation(r_buf[k][:], b0, ACT.Tanh, bias=bias[:, BR:BR + 1], scale=0.5)\
                        .then_inc(sig["r_tanh"][k], 1)
                if op == "R q_hi":
                    wait("rh")
                    copy("q_hi", q_hi[k][:], r_buf[k][:])
                if op == "U z_tanh":
                    wait("bank0")
                    act.activation(z_buf[k][:], b0, ACT.Tanh, bias=bias[:, BZ:BZ + 1], scale=0.5)\
                        .then_inc(sig["z_tanh"][k], 1)
                if op == "U v_tanh":
                    wait("bank1")
                    act.activation(v_buf[k][:], b1, ACT.Tanh, bias=bias[:, BV:BV + 1]).then_inc(sig["v_tanh"][k], 1)
                if op == "T n_hi":
                    wait("bank0")
                    copy("n_hi", n_hi[k][:], b0)
                if op == "T t_hi":
                    wait("h_new")
                    copy("t_hi", t_hi[k][:], hT[k][:])
                if op == "norm n_hi":
                    wait("normed")
                    copy("n_hi", n_hi[k][:], x_nat[k][:])
                if op == "ZT store":
                    wait("normed")
                    dst = out_rows[bass.ds(at.row(k), 1)].rearrange("a p c d -> (a p) c d")
                    act.dma_start(dst, x_nat[k][:]).then_inc(x_nat_free[k], 16)
                if op == "X t_hi":
                    wait("bank0")
                    copy("t_hi", t_hi[k][:], b0)
                if op == "XA m_hi":
                    wait("bank1")
                    copy("m_hi", m_hi[k][:], b1)
                if op == "Y hT":
                    wait("bank0")
                    copy("hT_copied", hT[k][:], b0)
                if op == "YT n_hi":
                    wait("bank0")
                    copy("n_hi", n_hi[k][:], b0)
                if op == "Z hT":
                    wait("bank1")
                    act.activation(hT[k][:], b1, ACT.Relu if layer == 1 else ACT.Identity,
                                   bias=cols[:, 5:6] if layer == 1 else cols[:, 6:7])\
                        .then_inc(sig["hT_copied"][k], 1)
                if op == "G q_hi":
                    wait("bank1")
                    copy("q_hi", q_hi[k][:], b1)
                if op == "S m_hi":
                    wait("masked")
                    if layer > 0:
                        act.wait_ge(sig["bank1"][k], at.before("bank1"))
                    copy("m_hi", m_hi[k][:], e_buf)
                if op == "S r_tanh":
                    if layer > 1:
                        act.wait_ge(sig["e_sum"][k], at.upto("e_sum", at.j - 2))
                    act.wait_ge(sig["bank0"][k], at.before("bank0"))
                    act.activation(e_buf, b0, ACT.Tanh, scale=SCORE).then_inc(sig["r_tanh"][k], 1)
                if op == "S s_exp":
                    wait("r_tanh")
                    act.activation(e_buf, e_buf, ACT.Exp, scale=8.0).then_inc(sig["s_exp"][k], 1)
                if op == "O m_hi":
                    wait("bank1")
                    copy("m_hi", m_hi[k][:], b1)
                if op == "V hT":
                    wait("bank1")
                    copy("hT_copied", hT[k][:], b1)

            schedule(act, GROUPS, order["act"], emit, late)

        @block.vector
        def _(dve):
            dve.memset(ones[:], 1.0).then_inc(consts_ready, 1)
            dve.memset(eps[:], EPS).then_inc(consts_ready, 1)
            dve.memset(neg_half[:], -0.5).then_inc(consts_ready, 1)
            dve.memset(zeros[:], 0.0).then_inc(consts_ready, 1)
            dve.wait_ge(w_loaded, 16 * 7)
            dve.tensor_tensor(w_sum[:, 0:P], w4_raw[:, 0:P], w4_raw[:, P:2 * P], ALU.add).then_inc(w_summed, 1)
            dve.tensor_tensor(w_sum[:, 3 * P:4 * P], w3_raw[:, 0:P], w3_raw[:, P:2 * P], ALU.add)\
                .then_inc(w_summed, 1)
            dve.tensor_tensor(w_sum[:, 2 * P:3 * P], w5_raw[:, 0:P], w5_raw[:, P:2 * P], ALU.add)\
                .then_inc(w_summed, 1)
            dve.wait_ge(w_summed, 3)
            dve.tensor_tensor(w_sum[:, P:2 * P], w_sum[:, 3 * P:4 * P], w_sum[:, 0:P], ALU.subtract)\
                .then_inc(w_summed, 1)
            for c in range(C):
                dve.wait_ge(adjT_hi_ready, c + 1)
                dve.tensor_tensor(adjT_lo[:, c, :], bank0[c][:], adjT_hi[:, c, :].bitcast(F32), ALU.subtract)\
                    .then_inc(adjT_lo_ready, 1)
            dve.wait_ge(w_hi_ready, 3)
            dve.scalar_tensor_tensor(w_lo[:, U5H, :], bank1[2][:, 0:P], 0.25, w_hi[:, U5H, :].bitcast(F32),
                                     ALU.mult, ALU.subtract).then_inc(w_lo_ready, 1)
            dve.scalar_tensor_tensor(w_lo[:, W4:U3 + 1, :], bank1[3][:].rearrange("p (w o) -> p w o", o=P), 0.5,
                                     w_hi[:, W4:U3 + 1, :].bitcast(F32), ALU.mult, ALU.subtract)\
                .then_inc(w_lo_ready, 1)
            dve.wait_ge(w_hi_ready, 4)
            dve.tensor_tensor(w_lo[:, QK, :], bank1[1][:, 0:P], w_hi[:, QK, :].bitcast(F32), ALU.subtract)\
                .then_inc(w_lo_ready, 1)

            dve.wait_ge(bias_loaded, 16 * 7)
            dve.tensor_tensor(cols[:, 9:10], cols[:, 1:2], cols[:, 3:4], ALU.add).then_inc(bias_steps, 1)
            dve.tensor_tensor(cols[:, 10:11], cols[:, 0:1], cols[:, 3:4], ALU.add).then_inc(bias_steps, 1)
            dve.tensor_tensor(bias[:, BV:BV + 1], cols[:, 2:3], cols[:, 4:5], ALU.add).then_inc(bias_steps, 1)
            dve.wait_ge(bias_steps, 2)
            dve.tensor_scalar(bias[:, BR:BR + 1], cols[:, 9:10], 0.5, None, ALU.mult).then_inc(bias_steps, 1)
            dve.tensor_scalar(bias[:, BZ:BZ + 1], cols[:, 10:11], 0.5, None, ALU.mult).then_inc(bias_steps, 1)

            def late(what, c):
                if what == "weights lo":
                    dve.wait_ge(w_hi_ready, 5)
                    dve.tensor_tensor(w_lo[:, T0:L2 + 1, :], late_w[:], w_hi[:, T0:L2 + 1, :].bitcast(F32),
                                      ALU.subtract).then_inc(w_lo_ready, 1)
                if what == "degree":
                    dve.wait_ge(diag_cleared, c + 1)
                    dve.tensor_reduce(deg[:, DEG, c:c + 1], A_f[:, c, :], AX_X, ALU.add).then_inc(dinv_steps, 1)
                if what == "positive":
                    dve.wait_ge(dinv_steps, DEGREES)
                    dve.tensor_scalar(deg[:, POSITIVE, :], deg[:, DEG, :], 0.0, None, ALU.is_gt)\
                        .then_inc(dinv_steps, 1)
                if what == "safe a":
                    dve.wait_ge(dinv_steps, IS_POSITIVE)
                    dve.tensor_scalar(deg[:, ZERO, :], deg[:, POSITIVE, :], -1.0, 1.0, ALU.mult, ALU.add)\
                        .then_inc(dinv_steps, 1)
                    dve.scalar_tensor_tensor(deg[:, SAFE, :], deg[:, DEG, :], 0.0, deg[:, POSITIVE, :],
                                             ALU.max, ALU.mult).then_inc(dinv_steps, 1)
                if what == "safe b":
                    dve.wait_ge(dinv_steps, SAFE_PARTS)
                    dve.tensor_tensor(deg[:, SAFE, :], deg[:, SAFE, :], deg[:, ZERO, :], ALU.add)\
                        .then_inc(dinv_steps, 1)
                if what == "dinv":
                    dve.wait_ge(pow_ready, 1)
                    dve.tensor_tensor(deg[:, DINV, :], deg[:, POW, :], deg[:, POSITIVE, :], ALU.mult)\
                        .then_inc(dinv_steps, 1)
                if what == "negative":
                    dve.wait_ge(dinv_steps, HAS_DINV)
                    dve.tensor_scalar(deg[:, NEG_DINV, :], deg[:, DINV, :], -1.0, None, ALU.mult)\
                        .then_inc(dinv_steps, 1)
                if what == "lap lo":
                    dve.wait_ge(lapT_hi_ready, c + 1)
                    dve.scalar_tensor_tensor(lapT_lo[:, c, :], A_f[:, c, :], deg[:, NEG_DINV, c:c + 1],
                                             lapT_hi[:, c, :].bitcast(F32), ALU.mult, ALU.subtract)\
                        .then_inc(lapT_lo_ready, 1)

            def emit(op, kind, layer, k, at):
                def wait(signal):
                    dve.wait_ge(sig[signal][k], at.now(signal))

                def low(signal, dst, src, hi):
                    dve.tensor_tensor(dst, src, hi.bitcast(F32), ALU.subtract).then_inc(sig[signal][k], 1)

                b0, b1 = bank0[k][:], bank1[k][:]
                e_buf = (r_buf, z_buf)[layer % 2][k][:]
                if op == "X0 t_lo":
                    wait("t_hi")
                    wait("hT_copied")
                    low("t_lo", t_lo[k][:], hT[k][:], t_hi[k][:])
                if op == "X0 n_lo":
                    wait("n_hi")
                    dve.scalar_tensor_tensor(n_lo[k][:], x_in[k][:], 2.0, n_hi[k][:].bitcast(F32),
                                             ALU.mult, ALU.subtract).then_inc(sig["n_lo"][k], 1)
                if op == "A m_lo":
                    wait("m_hi")
                    low("m_lo", m_lo[k][:], b1, m_hi[k][:])
                if op == "R q_lo":
                    wait("q_hi")
                    low("q_lo", q_lo[k][:], r_buf[k][:], q_hi[k][:])
                if op == "R rh":
                    wait("r_tanh")
                    dve.scalar_tensor_tensor(r_buf[k][:], r_buf[k][:], 1.0, hT[k][:], ALU.add, ALU.mult)\
                        .then_inc(sig["rh"][k], 1)
                if op == "U h_new":
                    wait("v_taken")
                    dve.scalar_tensor_tensor(hT[k][:], r_buf[k][:], -0.5, v_buf[k][:], ALU.mult, ALU.add)\
                        .then_inc(sig["h_new"][k], 1)
                if op == "U h_kept":
                    dve.wait_ge(sig["q_lo"][k], at.before("q_lo"))
                    wait("z_tanh")
                    dve.scalar_tensor_tensor(r_buf[k][:], z_buf[k][:], 1.0, hT[k][:], ALU.subtract, ALU.mult)\
                        .then_inc(sig["h_kept"][k], 1)
                if op == "U v_taken":
                    wait("v_tanh")
                    dve.scalar_tensor_tensor(v_buf[k][:], z_buf[k][:], 1.0, v_buf[k][:], ALU.add, ALU.mult)\
                        .then_inc(sig["v_taken"][k], 1)
                if op == "T n_lo":
                    wait("n_hi")
                    low("n_lo", n_lo[k][:], b0, n_hi[k][:])
                if op == "norm summed":
                    if kind == "TL" and not at.first:
                        dve.wait_ge(x_nat_free[k], at.batches(16, 0))
                    wait("bank0")
                    if kind == "VT":
                        for c in range(C):
                            mm = dve.scalar_tensor_tensor(x_nat[k][:, c, :], bank0[k][:, c * P:(c + 1) * P],
                                                          recip[k][:, c:c + 1], x_nat[k][:, c, :],
                                                          ALU.mult, ALU.add)
                    elif kind == "TL":
                        mm = dve.scalar_tensor_tensor(x_nat[k][:].rearrange("p c d -> p (c d)"), b0, 0.5,
                                                      x_in[k][:].rearrange("p c d -> p (c d)"), ALU.mult, ALU.add)
                    else:
                        mm = dve.tensor_tensor(x_nat[k][:], b0.rearrange("p (c d) -> p c d", c=C), x_nat[k][:], ALU.add)
                    mm.then_inc(sig["summed"][k], 1)
                if op == "norm stats":
                    wait("summed")
                    for c in range(C):
                        mm = dve.bn_stats(stats[k][:, c, :], x_nat[k][:, c, :])
                    mm.then_inc(sig["stats"][k], 1)
                if op == "norm moments":
                    wait("stats")
                    dve.tensor_copy(recip[k][:, 0:1], stats[k][:, 0, 1:2])
                    for c in range(C):
                        mm = dve.bn_aggr(moments[k][:, c, :], stats[k][:, c, :])
                    mm.then_inc(sig["moments"][k], 1)
                if op == "norm normed":
                    wait("rstd")
                    for c in range(C):
                        mm = dve.tensor_scalar(x_nat[k][:, c, :], x_nat[k][:, c, :], moments[k][:, c, 0:1],
                                               rstd[k][:, 1, c:c + 1], ALU.subtract, ALU.mult)
                    mm.then_inc(sig["normed"][k], 1)
                if op == "X t_lo":
                    wait("t_hi")
                    low("t_lo", t_lo[k][:], b0, t_hi[k][:])
                if op == "XA m_lo":
                    wait("m_hi")
                    low("m_lo", m_lo[k][:], b1, m_hi[k][:])
                if op == "YT n_lo":
                    wait("n_hi")
                    low("n_lo", n_lo[k][:], b0, n_hi[k][:])
                if op == "G q_lo":
                    wait("q_hi")
                    low("q_lo", q_lo[k][:], b1, q_hi[k][:])
                if op == "S masked":
                    wait("s_exp")
                    if at.first:
                        dve.wait_ge(adjT_ready, layer + 1)
                    dve.tensor_tensor(e_buf, e_buf, At_f[:, layer, :], ALU.mult)\
                        .then_inc(sig["masked"][k], 1)
                if op == "S m_lo":
                    wait("m_hi")
                    low("m_lo", m_lo[k][:], e_buf, m_hi[k][:])
                if op == "O m_lo":
                    wait("m_hi")
                    low("m_lo", m_lo[k][:], b1, m_hi[k][:])
                if op == "O recip":
                    wait("bank0")
                    dve.reciprocal(recip[k][:], bank0[k][:, 0:2 * C].rearrange("p (c t) -> p c t", t=2)[:, :, 0])\
                        .then_inc(sig["recip"][k], 1)

            schedule(dve, GROUPS, order["dve"], emit, late)

        @block.gpsimd
        def _(pool):
            pool.wait_ge(consts_ready, 1)
            pool.affine_select(out=ident[:], in_=ones[:], compare_op=ALU.is_equal, fill=0.0, base=0,
                               pattern=[[-1, P]], channel_multiplier=1).then_inc(ident_ready, 1)
            pool.wait_ge(consts_ready, 4)

            def late(what, c):
                def w(i):
                    return late_w[:, i - T0, :]

                def theta_raw(i):
                    return late_raw[:, i, :]

                def ws_raw(i):
                    return late_raw[:, 5 + i, :]

                def zero(n):
                    return zeros[:, 0:n]

                if what == "adj lo":
                    pool.wait_ge(adj_hi_ready, c + 1)
                    pool.tensor_tensor(adj_lo[:, c, :], A_f[:, c, :], adj_hi[:, c, :].bitcast(F32), ALU.subtract)\
                        .then_inc(adj_lo_ready, 1)
                if what == "weights a":
                    pool.wait_ge(late_loaded, 16 * 3)
                    pool.tensor_tensor(w(T2), theta_raw(2), theta_raw(4), ALU.add).then_inc(late_w_steps, 1)
                    pool.tensor_tensor(w(T1), theta_raw(1), theta_raw(3), ALU.add).then_inc(late_w_steps, 1)
                    pool.tensor_tensor(w(L0), ws_raw(0), ws_raw(2), ALU.subtract).then_inc(late_w_steps, 1)
                    pool.tensor_tensor(w(L2), ws_raw(2), ws_raw(2), ALU.add).then_inc(late_w_steps, 1)
                if what == "weights b":
                    pool.tensor_tensor(w(L1), ws_raw(1), zero(P), ALU.add).then_inc(late_w_steps, 1)
                    pool.tensor_tensor(w(VV), late_raw[:, 8, :], zero(P), ALU.add).then_inc(late_w_steps, 1)
                    pool.wait_ge(late_w_steps, 1)
                    pool.tensor_tensor(w(T0), theta_raw(0), w(T2), ALU.subtract).then_inc(late_w_steps, 1)
                    pool.wait_ge(late_w_steps, 7)
                    pool.tensor_tensor(w(T2), w(T2), w(T2), ALU.add).then_inc(late_w_steps, 1)
                if what == "diagonal":
                    pool.wait_ge(adj_lo_ready, c + 1)
                    pool.affine_select(out=A_f[:, c, :], in_=A_f[:, c, :], compare_op=ALU.not_equal, fill=0.0,
                                       base=c * P, pattern=[[-1, N]], channel_multiplier=1).then_inc(diag_cleared, 1)
                if what == "pow":
                    pool.wait_ge(dinv_steps, IS_SAFE)
                    pool.tensor_tensor(deg[:, POW, :], deg[:, SAFE, :], neg_half[:], ALU.pow).then_inc(pow_ready, 1)
                if what == "adjT":
                    pool.wait_ge(adjT_lo_ready, c + 1)
                    pool.tensor_tensor(At_f[:, c, :], adjT_hi[:, c, :].bitcast(F32), adjT_lo[:, c, :].bitcast(F32),
                                       ALU.add).then_inc(adjT_ready, 1)
                if what == "lap rows":
                    pool.wait_ge(adjT_ready, c + 1)
                    pool.wait_ge(dinv_moved, 32)
                    pool.tensor_tensor(A_f[:, c, :].rearrange("q (c p) -> q c p", p=P),
                                       At_f[:, c, :].rearrange("q (c p) -> q c p", p=P),
                                       dinv_row[:].rearrange("q p c -> q c p"), ALU.mult).then_inc(lap_rows_ready, 1)
                if what == "lap diagonal":
                    pool.wait_ge(lap_rows_ready, c + 1)
                    pool.affine_select(out=A_f[:, c, :], in_=A_f[:, c, :], compare_op=ALU.not_equal, fill=0.0,
                                       base=c * P, pattern=[[-1, N]], channel_multiplier=1).then_inc(lap_ready, 1)

            def emit(op, kind, layer, k, at):
                def wait(signal):
                    pool.wait_ge(sig[signal][k], at.now(signal))

                def low(signal, dst, src, hi):
                    pool.tensor_tensor(dst, src, hi.bitcast(F32), ALU.subtract).then_inc(sig[signal][k], 1)

                e_buf = (r_buf, z_buf)[layer % 2][k][:]
                if op == "T t_lo":
                    wait("t_hi")
                    low("t_lo", t_lo[k][:], hT[k][:], t_hi[k][:])
                if op == "norm var_eps":
                    wait("moments")
                    pool.tensor_tensor(rstd[k][:, 0, :], moments[k][:, :, 1], eps[:], ALU.add)\
                        .then_inc(sig["var_eps"][k], 1)
                if op == "norm rstd":
                    wait("var_eps")
                    pool.tensor_tensor(rstd[k][:, 1, :], rstd[k][:, 0, :], neg_half[:], ALU.pow)\
                        .then_inc(sig["rstd"][k], 1)
                if op == "norm n_lo":
                    wait("n_hi")
                    low("n_lo", n_lo[k][:], x_nat[k][:], n_hi[k][:])
                if op == "S e_sum":
                    wait("masked")
                    if layer == 0:
                        pool.tensor_tensor(v_buf[k][:], e_buf, zeros[:], ALU.add)\
                            .then_inc(sig["e_sum"][k], 1)
                    else:
                        pool.wait_ge(sig["e_sum"][k], at.before("e_sum"))
                        pool.tensor_tensor(v_buf[k][:], v_buf[k][:], e_buf, ALU.add)\
                            .then_inc(sig["e_sum"][k], 1)

            schedule(pool, GROUPS, order["pool"], emit, late)


_INS = ['x', 'adj', 'L0_gnn_w3_w', 'L0_gnn_w3_b', 'L0_gnn_u3_w', 'L0_gnn_u3_b', 'L0_gnn_w4_w', 'L0_gnn_w4_b',
        'L0_gnn_w5_w', 'L0_gnn_w5_b', 'L0_gnn_u5_w', 'L0_gnn_u5_b', 'L1_gnn_Theta1', 'L1_gnn_bias',
        'L2_gnn_q', 'L2_gnn_k', 'L2_gnn_v', 'L3_gnn_Ws', 'L3_gnn_bias']


def kernel(**inputs):
    import numpy as _np
    import concourse.bacc as _bacc
    from concourse import mybir as _mybir
    from concourse.bass_utils import run_bass_kernel_spmd as _run

    nc = _bacc.Bacc("TRN2", target_bir_lowering=False, num_devices=1)
    arrays, args = {}, []
    for name in _INS:
        a = _np.ascontiguousarray(inputs[name])
        arrays[f"in_{name}"] = a
        args.append(nc.dram_tensor(f"in_{name}", a.shape, _mybir.dt.from_np(a.dtype), kind="ExternalInput").ap())
    shape = _np.asarray(inputs['x']).shape
    args.append(nc.dram_tensor("out_0", shape, _mybir.dt.float32, kind="ExternalOutput").ap())
    resnorm_gnn(nc, *args)
    r = _run(nc, [arrays], core_ids=[0])
    return r.results[0]["out_0"]
```
